# Optimizing a Trainium2 kernel written in Bass

```python
import numpy as np
import jax
import jax.numpy as jnp

def _softmax(x, axis=-1):
    return jax.nn.softmax(x, axis=axis)

def _gelu(x):
    return jax.nn.gelu(x, approximate=True)

def _silu(x):
    return jax.nn.silu(x)

def _sigmoid(x):
    return jax.nn.sigmoid(x)

def _layernorm(x, axis=-1, eps=1e-05):
    m = jnp.mean(x, axis=axis, keepdims=True)
    v = jnp.var(x, axis=axis, keepdims=True)
    return (x - m) / jnp.sqrt(v + eps)

def _scatter_add(tgt, idx, src, axis=0):
    return tgt.at[idx].add(src)

def _segment_sum(src, seg, n):
    return jax.ops.segment_sum(src, seg, n)
kernel_name = 'mk_xattn_ffn_d2_seqx_r4_5df01b'

def setup_inputs(seed: int=0):
    np.random.seed(seed)
    _w = jnp.asarray

    def _rec_inputs():
        import jax
        import jax.numpy as jnp
        _rk = jax.random.key(seed)
        x = 7.22e-05 + 1 * jax.random.normal(jax.random.fold_in(_rk, 1), (2, 1024, 256), jnp.float32)
        _lenS = 1024 - jax.random.randint(jax.random.fold_in(_rk, 7), (2,), 0, max(1, 1024 // 4) + 1, jnp.int32)
        _lenS2 = 154 - jax.random.randint(jax.random.fold_in(_rk, 8), (2,), 0, max(1, 154 // 4) + 1, jnp.int32)
        _ctx_1024P = jax.random.normal(jax.random.fold_in(_rk, 11), (2, 16, 256), jnp.float32)
        _ctx_1024c = jax.random.dirichlet(jax.random.fold_in(_rk, 511), 0.3 * jnp.ones((16,), jnp.float32), (2, 154))
        _ctx_1024t = jnp.einsum('bsk,bkd->bsd', _ctx_1024c, _ctx_1024P)
        _ctx_1024t = _ctx_1024t * jax.lax.rsqrt(jnp.mean(jnp.square(_ctx_1024t)) + 1e-12) * 0.953939
        ctx_1024 = 4.13588e-05 + 0.999923 * (_ctx_1024t + 0.3 * jax.random.normal(jax.random.fold_in(_rk, 611), (2, 154, 256), jnp.float32))
        _validS = jnp.arange(1024)[None, :] < _lenS[:, None]
        _validS2 = jnp.arange(154)[None, :] < _lenS2[:, None]
        _causal = jnp.tril(jnp.ones((1024, 1024), dtype=bool))
        mask_SxS2_fk1 = jnp.where(jnp.broadcast_to(_validS2[0:1, :], (1024, 154)), 1.0, 0.0).astype(jnp.float32)
        return (x, ctx_1024, mask_SxS2_fk1)
    x, ctx_1024, mask_SxS2_fk1 = _rec_inputs()

    def _L0_xattn_setup():
        import jax, jax.numpy as jnp
        import numpy as np
        B, S, D = (4, 512, 256)
        key = jax.random.key(seed)
        ks = jax.random.split(key, 9)
        q = jax.random.normal(ks[0], (B, S, D), dtype=jnp.float32)
        k = jax.random.normal(ks[1], (B, S, D), dtype=jnp.float32)
        v = jax.random.normal(ks[2], (B, S, D), dtype=jnp.float32)
        sc = 1.0 / np.sqrt(D)
        Wq = jax.random.normal(ks[3], (D, D), dtype=jnp.float32) * sc
        Wk = jax.random.normal(ks[4], (D, D), dtype=jnp.float32) * sc
        Wv = jax.random.normal(ks[5], (D, D), dtype=jnp.float32) * sc
        bq = jnp.zeros((D,), dtype=jnp.float32)
        bk = jnp.zeros((D,), dtype=jnp.float32)
        bv = jnp.zeros((D,), dtype=jnp.float32)
        mask = jnp.triu(jnp.ones((S, S), dtype=jnp.float32), k=1)
        return {'q': q, 'k': k, 'v': v, 'mask': mask, 'Wq': Wq, 'bq': bq, 'Wk': Wk, 'bk': bk, 'Wv': Wv, 'bv': bv}
    _L0_xattn_all = _L0_xattn_setup()
    _L0_xattn_in = {k: v for k, v in _L0_xattn_all.items() if k in ('Wq', 'bq', 'Wk', 'bk', 'Wv', 'bv')}
    del _L0_xattn_all

    def _L0_ffn_setup():
        import jax, jax.numpy as jnp
        import numpy as np
        E = 16
        H = 256
        F = 512
        TOP_K = 1
        B, S = (2, 256)
        key = jax.random.key(seed)
        ks = jax.random.split(key, 7)
        s = 0.02
        return {'hidden_states': jax.random.normal(ks[0], (B, S, H), jnp.float32), 'w_router': jax.random.normal(ks[1], (E, H), jnp.float32) * s, 'gate_up_proj': jax.random.normal(ks[2], (E, H, 2 * F), jnp.float32) * s, 'down_proj': jax.random.normal(ks[3], (E, F, H), jnp.float32) * s, 'w_gate': jax.random.normal(ks[4], (F, H), jnp.float32) * s, 'w_up': jax.random.normal(ks[5], (F, H), jnp.float32) * s, 'w_down': jax.random.normal(ks[6], (H, F), jnp.float32) * s}
    _L0_ffn_all = _L0_ffn_setup()
    _L0_ffn_in = {k: v for k, v in _L0_ffn_all.items() if k in ('w_router', 'gate_up_proj', 'down_proj', 'w_gate', 'w_up', 'w_down')}
    del _L0_ffn_all

    def _L1_xattn_setup():
        import jax, jax.numpy as jnp
        import numpy as np
        EMBED = 256
        HEADS = 16
        HEAD_DIM = EMBED // HEADS
        EXP_DIM = 2 * HEAD_DIM

        def _feature_map(x, fm_w, fm_b):
            z = jnp.einsum('nshd,ed->nshe', x, fm_w) + fm_b
            return jnp.concatenate([jnp.exp(z), jnp.exp(-z)], axis=-1)
        key = jax.random.key(seed)
        ks = jax.random.split(key, 7)
        N, S = (4, 512)
        values = jax.random.normal(ks[0], (N, S, EMBED), dtype=jnp.float32)
        keys_ = jax.random.normal(ks[1], (N, S, EMBED), dtype=jnp.float32)
        query = jax.random.normal(ks[2], (N, S, EMBED), dtype=jnp.float32)
        fm_w = jnp.eye(HEAD_DIM, dtype=jnp.float32) + 0.02 * jax.random.normal(ks[3], (HEAD_DIM, HEAD_DIM), dtype=jnp.float32)
        fm_b = 0.02 * jax.random.normal(ks[4], (HEAD_DIM,), dtype=jnp.float32)
        fc_w = jax.random.normal(ks[5], (EMBED, HEADS * EXP_DIM), dtype=jnp.float32) * (1.0 / np.sqrt(HEADS * EXP_DIM))
        fc_b = jnp.zeros((EMBED,), dtype=jnp.float32)
        return {'values': values, 'keys': keys_, 'query': query, 'fm_w': fm_w, 'fm_b': fm_b, 'fc_w': fc_w, 'fc_b': fc_b}
    _L1_xattn_all = _L1_xattn_setup()
    _L1_xattn_in = {k: v for k, v in _L1_xattn_all.items() if k in ('fm_w', 'fm_b', 'fc_w', 'fc_b')}
    del _L1_xattn_all

    def _L1_ffn_setup():
        import jax, jax.numpy as jnp
        import numpy as np
        TOP_K = 8
        key = jax.random.key(seed)
        ks = jax.random.split(key, 6)
        B, S, D, F, E = (2, 256, 256, 128, 64)
        x = jax.random.normal(ks[0], (B, S, D), dtype=jnp.float32)
        centroids = jax.random.normal(ks[1], (E, D), dtype=jnp.float32) * 0.05
        expert_biases = jnp.zeros((E,), dtype=jnp.float32)
        Ws_up = jax.random.normal(ks[2], (D, F), dtype=jnp.float32) / np.sqrt(D)
        Ws_down = jax.random.normal(ks[3], (F, D), dtype=jnp.float32) / np.sqrt(F)
        W_up = jax.random.normal(ks[4], (E, D, F), dtype=jnp.float32) / np.sqrt(D)
        W_down = jax.random.normal(ks[5], (E, F, D), dtype=jnp.float32) / np.sqrt(F)
        return {'x': x, 'centroids': centroids, 'expert_biases': expert_biases, 'Ws_up': Ws_up, 'Ws_down': Ws_down, 'W_up': W_up, 'W_down': W_down}
    _L1_ffn_all = _L1_ffn_setup()
    _L1_ffn_in = {k: v for k, v in _L1_ffn_all.items() if k in ('centroids', 'expert_biases', 'Ws_up', 'Ws_down', 'W_up', 'W_down')}
    del _L1_ffn_all
    return {'x': x, 'ctx_1024': ctx_1024, 'mask_SxS2_fk1': mask_SxS2_fk1, 'L0_xattn_Wq': _L0_xattn_in['Wq'], 'L0_xattn_bq': _L0_xattn_in['bq'], 'L0_xattn_Wk': _L0_xattn_in['Wk'], 'L0_xattn_bk': _L0_xattn_in['bk'], 'L0_xattn_Wv': _L0_xattn_in['Wv'], 'L0_xattn_bv': _L0_xattn_in['bv'], 'L0_ffn_w_router': _L0_ffn_in['w_router'], 'L0_ffn_gate_up_proj': _L0_ffn_in['gate_up_proj'], 'L0_ffn_down_proj': _L0_ffn_in['down_proj'], 'L0_ffn_w_gate': _L0_ffn_in['w_gate'], 'L0_ffn_w_up': _L0_ffn_in['w_up'], 'L0_ffn_w_down': _L0_ffn_in['w_down'], 'L1_xattn_fm_w': _L1_xattn_in['fm_w'], 'L1_xattn_fm_b': _L1_xattn_in['fm_b'], 'L1_xattn_fc_w': _L1_xattn_in['fc_w'], 'L1_xattn_fc_b': _L1_xattn_in['fc_b'], 'L1_ffn_centroids': _L1_ffn_in['centroids'], 'L1_ffn_expert_biases': _L1_ffn_in['expert_biases'], 'L1_ffn_Ws_up': _L1_ffn_in['Ws_up'], 'L1_ffn_Ws_down': _L1_ffn_in['Ws_down'], 'L1_ffn_W_up': _L1_ffn_in['W_up'], 'L1_ffn_W_down': _L1_ffn_in['W_down']}

def reference(x, ctx_1024, mask_SxS2_fk1, L0_xattn_Wq, L0_xattn_bq, L0_xattn_Wk, L0_xattn_bk, L0_xattn_Wv, L0_xattn_bv, L0_ffn_w_router, L0_ffn_gate_up_proj, L0_ffn_down_proj, L0_ffn_w_gate, L0_ffn_w_up, L0_ffn_w_down, L1_xattn_fm_w, L1_xattn_fm_b, L1_xattn_fc_w, L1_xattn_fc_b, L1_ffn_centroids, L1_ffn_expert_biases, L1_ffn_Ws_up, L1_ffn_Ws_down, L1_ffn_W_up, L1_ffn_W_down):
    import jax
    import jax.numpy as jnp

    def _L0_xattn_ref(q, k, v, mask, Wq, bq, Wk, bk, Wv, bv):
        import jax, jax.numpy as jnp
        import numpy as np
        B, S, D = (4, 512, 256)
        WQ = q @ Wq + bq
        WK = k @ Wk + bk
        WV = v @ Wv + bv
        d_k = jnp.asarray(WK.shape[-1], dtype=jnp.float32)
        scores = jnp.einsum('bqd,bkd->bqk', WQ, WK) / jnp.sqrt(d_k)
        scores = scores + mask * -1000000000.0
        attn = jax.nn.softmax(scores, axis=-1)
        return jnp.einsum('bqk,bkd->bqd', attn, WV)

    def _L0_ffn_ref(hidden_states, w_router, gate_up_proj, down_proj, w_gate, w_up, w_down):
        import jax, jax.numpy as jnp
        import numpy as np
        E = 16
        H = 256
        F = 512
        TOP_K = 1
        B, S = (2, 256)
        b, s, h = hidden_states.shape
        x = hidden_states.reshape(-1, h)
        logits = x @ w_router.T
        _, top_idx = jax.lax.top_k(logits, TOP_K)
        mask = jax.nn.one_hot(top_idx, E, dtype=logits.dtype).sum(axis=1)
        scores = jax.nn.sigmoid(logits) * mask
        masked_inputs = scores.T[:, :, None] * x[None, :, :]
        gate_up = jnp.einsum('eth,ehf->etf', masked_inputs, gate_up_proj)
        gate, up = jnp.split(gate_up, 2, axis=-1)
        expert_out = jnp.einsum('etf,efh->eth', up * jax.nn.silu(gate), down_proj)
        shared = jax.nn.silu(x @ w_gate.T) * (x @ w_up.T) @ w_down.T
        out = shared + expert_out.sum(axis=0)
        return out.reshape(b, s, h)

    def _L1_xattn_ref(values, keys, query, fm_w, fm_b, fc_w, fc_b):
        import jax, jax.numpy as jnp
        import numpy as np
        EMBED = 256
        HEADS = 16
        HEAD_DIM = EMBED // HEADS
        EXP_DIM = 2 * HEAD_DIM

        def _feature_map(x, fm_w, fm_b):
            z = jnp.einsum('nshd,ed->nshe', x, fm_w) + fm_b
            return jnp.concatenate([jnp.exp(z), jnp.exp(-z)], axis=-1)
        N, S, _ = query.shape
        v = values.reshape(N, -1, HEADS, HEAD_DIM)
        k = keys.reshape(N, -1, HEADS, HEAD_DIM)
        q = query.reshape(N, -1, HEADS, HEAD_DIM)
        v, k, q = (_feature_map(x, fm_w, fm_b) for x in (v, k, q))
        scores = jnp.einsum('nqhd,nkhd->nhqk', q, k) / jnp.sqrt(jnp.float32(EMBED))
        attn = jax.nn.softmax(scores, axis=-1)
        out = jnp.einsum('nhql,nlhd->nqhd', attn, v)
        out = out.reshape(N, S, HEADS * EXP_DIM)
        return out @ fc_w.T + fc_b

    def _L1_ffn_ref(x, centroids, expert_biases, Ws_up, Ws_down, W_up, W_down):
        import jax, jax.numpy as jnp
        import numpy as np
        TOP_K = 8
        B, S, D = x.shape
        E = centroids.shape[0]
        T = B * S
        xf = x.reshape(T, D)
        shared = jax.nn.silu(xf @ Ws_up) @ Ws_down
        aff = xf @ centroids.T
        biased = aff + expert_biases
        _, idx = jax.lax.top_k(biased, TOP_K)
        sel = jnp.take_along_axis(aff, idx, axis=1)
        w = jax.nn.sigmoid(sel)
        w = w / (jnp.sum(w, axis=-1, keepdims=True) + 1e-08)
        cw = jnp.zeros((T, E), dtype=x.dtype).at[jnp.arange(T)[:, None], idx].add(w)
        h = jax.nn.silu(jnp.einsum('td,edf->etf', xf, W_up))
        y = jnp.einsum('etf,efd->etd', h, W_down)
        routed = jnp.einsum('etd,te->td', y, cw)
        return (shared + routed).reshape(B, S, D)
    x = x + _L0_xattn_ref(_layernorm(x, axis=-1), ctx_1024, ctx_1024, mask_SxS2_fk1, L0_xattn_Wq, L0_xattn_bq, L0_xattn_Wk, L0_xattn_bk, L0_xattn_Wv, L0_xattn_bv)
    x = x + _L0_ffn_ref(_layernorm(x, axis=-1), L0_ffn_w_router, L0_ffn_gate_up_proj, L0_ffn_down_proj, L0_ffn_w_gate, L0_ffn_w_up, L0_ffn_w_down)
    x = x + _L1_xattn_ref(ctx_1024, ctx_1024, _layernorm(x, axis=-1), L1_xattn_fm_w, L1_xattn_fm_b, L1_xattn_fc_w, L1_xattn_fc_b)
    x = x + _L1_ffn_ref(_layernorm(x, axis=-1), L1_ffn_centroids, L1_ffn_expert_biases, L1_ffn_Ws_up, L1_ffn_Ws_down, L1_ffn_W_up, L1_ffn_W_down)
    return x

_drawn_inputs = setup_inputs


def setup_inputs(seed=0):
    import zlib

    import numpy as np

    out = dict(_drawn_inputs(seed))
    spreads = {'L0_xattn_bq': (0.0, 0.312),
     'L0_xattn_bk': (0.0, 2.0),
     'L0_xattn_bv': (0.0, 0.1),
     'L1_xattn_fc_b': (0.0, 0.8),
     'L1_ffn_expert_biases': (0.0, 0.8)}
    factors = {'L0_ffn_w_router': 5.532,
     'L0_ffn_gate_up_proj': 5.964,
     'L0_ffn_down_proj': 5.677,
     'L1_ffn_centroids': 3.539,
     'L1_ffn_W_up': 3.5,
     'L1_ffn_W_down': 3.216,
     'L0_ffn_w_gate': 3.159,
     'L0_ffn_w_up': 3.187,
     'L0_ffn_w_down': 3.253}
    for name, (base, spread) in spreads.items():
        noise = np.random.default_rng([zlib.crc32(name.encode()), seed]).standard_normal(out[name].shape)
        drawn = base * np.exp(spread * noise) if base else spread * noise
        out[name] = jnp.asarray(drawn.astype(out[name].dtype))
    for name, factor in factors.items():
        out[name] = (out[name] * factor).astype(out[name].dtype)
    return out
```

```python
from contextlib import ExitStack

import concourse.bass as bass
from concourse import mybir

F32 = mybir.dt.float32
F16 = mybir.dt.float16
I32 = mybir.dt.int32
U32 = mybir.dt.uint32
ALU = mybir.AluOpType
ACT = mybir.ActivationFunctionType
X_AXIS = mybir.AxisListType.X

P = 128
BANK = 512
LN_EPS = 1e-5
MASKED = -1000000000.0


def build(nc, x, ctxT, mask, WqT, bq, Wk, bk, Wv, bv, w_routerT, gate_up, down, w_gateT, w_upT, w_downT,
          fm_wT, fm_b, fc_wT, fc_b, centroidsT, expert_biases, Ws_up, Ws_down, W_up, W_down, out):
    TOK, D = x.shape
    NB, _, S2 = ctxT.shape
    NT = TOK // P
    TPB = NT // NB
    KC = D // P
    SL = S2 - P
    QS = float(D) ** -0.5
    E0, _, F2 = gate_up.shape
    F0 = F2 // 2
    FC0 = F0 // P
    E1, _, F1 = W_up.shape
    TOP1 = 8
    HD = fm_b.shape[0]
    NH = D // HD
    FD = 2 * HD
    HG = P // FD
    NG = NH // HG
    VW = FD + 1
    NX0 = 32
    NX1 = 192
    assert NX0 >= E0 - 1 + TOK // P and NX1 >= E1 - 1 + TOK * TOP1 // P
    RING = 8
    GROUPS0, GROUPS1 = NX0 // RING, NX1 // RING

    scaled0 = nc.dram_tensor("scaled0", [TOK, D], F32).ap()
    routed0 = nc.dram_tensor("routed0", [NX0 * P, D], F32).ap()
    normed1 = nc.dram_tensor("normed1", [TOK, D], F32).ap()
    routed1 = nc.dram_tensor("routed1", [NX1 * P, D], F32).ap()

    ctx = ExitStack()
    with ctx:
        def sb(name, shape, dt=F32):
            return ctx.enter_context(nc.sbuf_tensor(name, shape, dt))

        sems = {}

        STEPS = {}
        for shared, names in (
            ("attention0_psum", ("xn1T_ps", "s0_ps", "p0T_ps", "attn0_ps", "xn2T_ps")),
            ("ffn0_psum", ("lg0_ps", "gate0_ps", "up0_ps", "rank0_ps", "ffn0_ps")),
            ("softmax0_steps", ("s0", "nm0", "rinv0")),
            ("norm2_steps", ("x1", "stats2", "mv2", "var2", "xn2")),
            ("router0_steps", ("lg0", "best0", "best_i0", "top0", "sel0", "sgd0", "score0", "xs0")),
            ("hidden0_steps", ("ha0", "h0")),
            ("counts0_steps", ("rank0", "sel_sum0")),
            ("projection1_psum", ("ofT_ps", "fc_ps", "xn4T_ps", "lg1_ps", "ffn1_ps", "rank1_ps")),
            ("query1_psum", ("xn3T_ps", "qf_ps")),
            ("norm3_steps", ("x2", "stats3", "mv3", "var3", "xn3", "x2b")),
            ("norm4_steps", ("x3", "stats4", "mv4", "var4", "xn4")),
            ("router1_steps", ("aff", "hs1", "biased", "best1", "rep1", "sel1")),
            ("weights1_steps", ("w_sig", "w_rec", "w_sum", "w_sume", "w_inv", "weight")),
            ("counts1_steps", ("rank1", "sel_sum1")),
            ("route_psum", ("count_ps", "base_ps", "end_ps", "row_ps")),
            ("route_steps", ("count", "ntiles", "end", "key_all", "key", "slot_i", "hi_i", "hi", "lo_", "lo")),
        ):
            for i, name in enumerate(names):
                STEPS[name] = (shared, i + 1, len(names))
        AHEAD = ("projection1_psum", "router1_steps", "weights1_steps")

        def start_ahead(eng, shared):
            eng.sem_inc(S(shared), next(steps for name, (of, _, steps) in STEPS.items() if of == shared))

        def S(name):
            name = STEPS[name][0] if name in STEPS else name
            if name not in sems:
                sems[name] = ctx.enter_context(nc.semaphore(name))
            return sems[name]

        def nth(name, n):
            shared, step, steps = STEPS[name]
            return n * steps + (step if shared in AHEAD else step - steps)

        def some(n):
            return not (isinstance(n, int) and n <= 0)


        X = sb("X", [P, NT, D])
        ident = sb("ident", [P, P])
        tri = sb("tri", [P, P], F16)
        triinc = sb("triinc", [P, P], F16)
        ones16 = sb("ones16", [P, P], F16)
        ones_row = sb("ones_row", [1, P])
        iota16 = sb("iota16", [P, NX1], F16)
        step128 = sb("step128", [P, NT])
        token_id = sb("token_id", [P, NT])
        neg_half = sb("neg_half", [P, NT])
        stats = sb("stats", [P, 6])
        mv_all = sb("mv_all", [P, NT, 2])
        rstd_all = sb("rstd_all", [P, NT])
        mv = sb("mv", [P, 2])
        var_eps = sb("var_eps", [P, 1])
        rstd = sb("rstd", [P, 1])
        small = sb("small", [P, 64])
        rank = sb("rank", [P, NT, E1])
        sel = sb("sel", [P, NT, E1], F16)
        weight = sb("weight", [P, NT, E1])
        sel_sum = sb("sel_sum", [P, E1], F16)
        tiles_of = sb("tiles_of", [P, 4])
        tiles16 = sb("tiles16", [P, 1 + P], F16)
        ended = sb("ended", [P, NX1], F16)
        base = sb("base", [P, E1])
        slots = sb("slots", [P, NT * TOP1])
        slot_i = sb("slot_i", [P, NT * TOP1], I32)
        tmp_i = sb("tmp_i", [P, NT * TOP1], I32)
        slot_hi = sb("slot_hi", [P, NT * TOP1])
        slot_lo = sb("slot_lo", [P, NT * TOP1])
        w_slot = sb("w_slot", [P, NT * TOP1])
        token_of = sb("token_of", [P, NX1], I32)
        expert_of = sb("expert_of", [1, NX1], I32)
        idx8 = sb("idx8", [P, 2, RING], I32)
        idx1 = sb("idx1", [P, 1], I32)
        head_of = sb("head_of", [P, HG])

        den = sb("den", [P, 2 * HG])
        lg = sb("lg", [P, E1])
        lg2 = sb("lg2", [P, E1])
        best = sb("best", [P, 8])
        best_i = sb("best_i", [P, 8], U32)
        rsum = sb("rsum", [P, 1])
        rinv = sb("rinv", [P, 1])
        nm0 = sb("nm0", [P, 1])
        sg_e = sb("sg_e", [P, E1])
        sg_d = sb("sg_d", [P, E1])
        wsum = sb("wsum", [P, 2])
        nmax2 = sb("nmax2", [P, 2, HG])

        R = sb("R", [P, E1 * KC * P + E1 * D])
        Q = sb("Q", [P, 11204])

        def carver(region, at=0):
            where = [at]

            def take(*dims):
                n = 1
                for d in dims:
                    n *= d
                v = region[:, where[0]:where[0] + n]
                where[0] += n
                if len(dims) == 2:
                    v = v.rearrange("p (a b) -> p a b", a=dims[0])
                if len(dims) == 3:
                    v = v.rearrange("p (a b c) -> p a b c", a=dims[0], b=dims[1])
                if len(dims) == 4:
                    v = v.rearrange("p (a b c d) -> p a b c d", a=dims[0], b=dims[1], c=dims[2])
                return v
            return take

        r = carver(R)
        expert_gu = [r(KC, F2) for _ in range(2)]
        expert_dn = [r(FC0, D) for _ in range(2)]
        wg, wu, wd = r(KC, F0), r(KC, F0), r(FC0, D)
        wr = r(KC, E0)
        cT = r(NB, KC, S2)
        cL = r(NB, KC, SL * HG)
        wk, wq, wv = r(KC, D), r(KC, D), r(KC, D)
        bkc, bqc, bvb = r(KC), r(KC), r(D)
        kT = r(NB, KC, S2)
        qk = r(NB, KC, S2)
        bqk = r(NB, S2)
        v0 = r(NB, 2, D)
        msk = r(TPB, S2)
        xn1, xn1T, s0, p0, p0T = r(D), r(KC, P), r(S2), r(2, P), r(2, P)
        xn2, xn2T, xs0 = r(D), r(KC, P), r(D)
        th0, a0, h0 = r(F0), r(F0), r(FC0, P)
        g0, y0 = r(RING, D), r(RING, D)
        x0T, sg0, e0T = r(2, KC, P), r(2, F0), r(2, FC0, P)
        key0 = r(NT, E0)
        head_at = r(HG, SL)
        one_lo0 = r(4 * P // 2).bitcast(F16).rearrange("p (k n) -> p k n", k=4)
        one_hi0 = r(4 * NX0 // 2).bitcast(F16).rearrange("p (k n) -> p k n", k=4)

        NUP = E1 * KC * F1
        w_up1 = R[:, 0:NUP].rearrange("p (e c f) -> p e c f", e=E1, c=KC)
        w_dn1 = R[:, NUP:NUP + E1 * D].rearrange("p (e d) -> p e d", e=E1)
        LATE = 16
        r = carver(R, NUP + (E1 - LATE) * D)
        prob = r(2, S2 * HG)
        probT, leftT = r(2, HG, P), r(2, P)
        of, ofT = r(NH, FD), r(NG, P)
        th1, hs1T = r(P), r(P)
        q = carver(Q)
        kbd, vb, vl = q(NB, NH, S2), q(NB, NH, VW), q(NB, NH, VW)
        fcw, wsu, wsd, cen = q(NG, D), q(KC, F1), q(D), q(KC, E1)
        fcb, ebb = q(D), q(E1)
        fm2, fmr, fmc = q(2, P), q(P), q(1)
        yg, xn3, xn3T, qf = q(D), q(D), q(KC, P), q(NG, P)
        xn4, xn4T = q(D), q(KC, P)
        q = carver(Q)
        g1, y1 = q(RING, D), q(RING, D)
        x1T, h1, h1T = q(2, KC, P), q(2, F1), q(2, P)
        cg = q(2, TOP1, D)
        slot_key = q(NT, E1)
        slot_junk = q(TOP1, E1)
        q = carver(Q)
        one_lo1 = q(4 * P // 2).bitcast(F16).rearrange("p (k n) -> p k n", k=4)
        one_hi1 = q(4 * NX1 // 2).bitcast(F16).rearrange("p (k n) -> p k n", k=4)

        PS = ctx.enter_context(nc.psum_tensor("PS", [P, 8, BANK], F32))

        def bank(b):
            return PS[:, b, :]

        x_t = x.rearrange("(t p) d -> p t d", p=P)
        out_t = out.rearrange("(t p) d -> t p d", p=P)
        block = ctx.enter_context(nc.Block())

        def chunks(a):
            return a.rearrange("(c p) n -> p c n", p=P)

        def tile_loop(eng, body):
            body(0)
            with eng.Fori(1, NT - 1, 1) as t:
                body(t)
            body(NT - 1)

        def group_loop(eng, groups, body):
            body(0)
            with eng.Fori(1, groups - 1, 1) as n:
                body(n)
            body(groups - 1)

        def row(ap, t):
            return ap[:, bass.ts(t, 1), :].rearrange("p a d -> p (a d)")

        @block.sync
        def _(sp):
            for b in range(NB):
                sp.dma_start(cT[:, b], chunks(ctxT[b])).then_inc(S("ctx_in"), 16)
            for dst, src in ((wk, Wk), (wq, WqT), (wv, Wv)):
                sp.dma_start(dst, chunks(src)).then_inc(S("ctx_in"), 16)
            sp.dma_start(bkc, bk).then_inc(S("ctx_in"), 16)
            sp.dma_start(bqc, bq).then_inc(S("ctx_in"), 16)
            sp.dma_start(bvb, bv.partition_broadcast(P)).then_inc(S("ctx_in"), 16)
            sp.dma_start(msk, mask.rearrange("(t p) k -> p t k", p=P)).then_inc(S("mask_in"), 16)
            for dst, src in ((wr, w_routerT), (wg, w_gateT), (wu, w_upT), (wd, w_downT)):
                sp.dma_start(dst, chunks(src)).then_inc(S("ffn0_in"), 16)
            for dst, src in ((fcw, fc_wT), (wsu, Ws_up), (cen, centroidsT)):
                sp.dma_start(dst, chunks(src)).then_inc(S("small1_in"), 16)
            sp.dma_start(wsd, Ws_down).then_inc(S("small1_in"), 16)
            sp.dma_start(fcb, fc_b.partition_broadcast(P)).then_inc(S("small1_in"), 16)
            sp.dma_start(ebb, expert_biases.partition_broadcast(P)).then_inc(S("small1_in"), 16)
            sp.wait_ge(S("zeroed"), 1)
            for h in range(P // HD):
                dst = fm2[HD * h:HD * h + HD, h // HG, FD * (h % HG):FD * (h % HG) + HD]
                sp.dma_start(dst, fm_wT).then_inc(S("fm_in"), 16)
                sp.dma_start(fmr[0:1, HD * h:HD * h + HD], fm_b.rearrange("(a e) -> a e", a=1)).then_inc(S("fm_in"), 16)

            def store0(t):
                sp.wait_ge(S("xs0"), nth("xs0", t + 1))
                sp.dma_start(scaled0[bass.ts(t, P), :], xs0).then_inc(S("xs0_stored"), 16)
            store0(0)
            with sp.Fori(1, NT, 1) as t:
                store0(t)

            sp.wait_ge(S("expert_row"), 1)

            def load0(n, k):
                j = n * RING + k
                if some(j - 1):
                    sp.wait_ge(S("dn0"), j - 1)
                e = sp.value_load(expert_of[0:1, bass.ts(j, 1)], min_val=0, max_val=E0 - 1)
                sp.dma_start(expert_gu[k % 2], gate_up[bass.ts(e, 1), :, :].rearrange("a (c p) f -> p (a c) f", p=P)).then_inc(S(f"gu_in{k % 2}"), 16)
                sp.dma_start(expert_dn[k % 2], down[bass.ts(e, 1), :, :].rearrange("a (c p) f -> p (a c) f", p=P)).then_inc(S(f"dn_in{k % 2}"), 16)

            def out0(n, k):
                sp.wait_ge(S("y0"), n * RING + k + 1)
                sp.dma_start(routed0[bass.ts(n * RING + k, P), :], y0[:, k]).then_inc(S(f"rows_out{k}"), 16)

            def experts0(n):
                for k in range(RING):
                    load0(n, k)
                    if k >= 2:
                        out0(n, k - 2)
                    elif not (isinstance(n, int) and n == 0):
                        out0(n - 1, k + RING - 2)
            group_loop(sp, GROUPS0, experts0)
            out0(GROUPS0 - 1, RING - 2)
            out0(GROUPS0 - 1, RING - 1)

            sp.wait_ge(S("y0"), NX0)
            for k in range(RING):
                sp.wait_ge(S(f"rows_out{k}"), 16 * GROUPS0)
            sp.wait_ge(S("setup1_done"), 1)
            EB = 8

            def store1(t):
                sp.wait_ge(S("xn4"), nth("xn4", t + 1))
                sp.dma_start(normed1[bass.ts(t, P), :], xn4).then_inc(S("xn4_stored"), 16)
            ups, downs = E1 // EB, (E1 - LATE) // EB
            with sp.Fori(0, ups, 1) as t:
                store1(t)
                for c in range(KC):
                    sp.dma_start(w_up1[:, bass.ts(t, EB), c], W_up[bass.ts(t, EB), c * P:(c + 1) * P].rearrange("e p f -> p e f")).then_inc(S("w1_in"), 16)
            with sp.Fori(0, downs, 1) as i:
                store1(i + ups)
                sp.dma_start(w_dn1[:, bass.ts(i, EB)], W_down[bass.ts(i, EB)].rearrange("e f d -> f e d")).then_inc(S("w1_in"), 16)
            with sp.Fori(ups + downs, NT, 1) as t:
                store1(t)
            sp.wait_ge(S("attention1_done"), 1)
            for e in range(E1 - LATE, E1, EB):
                sp.dma_start(w_dn1[:, e:e + EB], W_down[e:e + EB].rearrange("e f d -> f e d")).then_inc(S("w1_in"), 16)

            def experts1(n):
                for k in range(RING):
                    sp.wait_ge(S("y1"), n * RING + k + 1)
                    sp.dma_start(routed1[bass.ts(n * RING + k, P), :], y1[:, k]).then_inc(S(f"rows_out{k}"), 16)
            group_loop(sp, GROUPS1, experts1)

            def store_out(t):
                sp.wait_ge(S("final"), t + 1)
                sp.dma_start(out_t[bass.ts(t, 1)].rearrange("a p d -> (a p) d"), row(X, t)).then_inc(S("out_stored"), 16)
            with sp.Fori(0, NT, 1) as t:
                store_out(t)
            sp.wait_ge(S("out_stored"), 16 * NT)

        def route_tensor(pe, one_lo, one_hi, E, NX, pairs, L):
            pe.wait_ge(S("sel_total"), L + 1)
            pe.matmul(bank(0)[0:E, 0:1], sel_sum[:, 0:E], ones16[:, 0:1], start=True, stop=True).then_inc(S("count_ps"), 1)
            pe.wait_ge(S("tiles"), 2 * (L + 1))
            pe.matmul(bank(1)[:, 0:E], tiles16[0:E, 1:1 + P], tri[0:E, 0:E], start=True, stop=True).then_inc(S("base_ps"), 1)
            pe.matmul(bank(2)[0:E, 0:1], triinc[0:E, 0:E], tiles16[0:E, 0:1], start=True, stop=True).then_inc(S("end_ps"), 1)
            pe.wait_ge(S("ended"), L + 1)
            pe.matmul(bank(3)[0:1, 0:NX], ones16[0:E, 0:1], ended[0:E, 0:NX], start=True, stop=True).then_inc(S("row_ps"), 1)

            def pair4(i, first, last):
                for k in range(4):
                    pe.wait_ge(S("one_hi"), NT * L + 4 * i + k + 1)
                    pe.matmul(bank(4)[:, 0:NX], one_lo[:, k, :], one_hi[:, k, 0:NX],
                              start=first and k == 0, stop=last and k == 3).then_inc(S("pair"), 1)
            n = pairs // 4
            pair4(0, True, False)
            with pe.Fori(1, n - 1, 1) as i:
                pair4(i, False, False)
            pair4(n - 1, False, True)

        def route_vector(dve, key, one_lo, one_hi, E, NX, per, L):
            n = NT * per
            dve.wait_ge(S("count_ps"), nth("count_ps", L + 1))
            dve.tensor_copy(tiles_of[0:E, 0:1], bank(0)[0:E, 0:1]).then_inc(S("count"), 1)
            dve.wait_ge(S("count"), nth("count", L + 1))
            dve.tensor_scalar(small[0:E, 0:NT], step128[0:E, :], tiles_of[0:E, 0:1], 0.0, ALU.is_lt, ALU.add,
                              accum_out=tiles_of[0:E, 1:2]).then_inc(S("ntiles"), 1)
            dve.wait_ge(S("ntiles"), nth("ntiles", L + 1))
            dve.tensor_copy(tiles16[0:E, 0:1], tiles_of[0:E, 1:2]).then_inc(S("tiles"), 1)
            dve.tensor_scalar(tiles16[0:E, 1:1 + P], ones16[0:E, :], tiles_of[0:E, 1:2], None, ALU.mult).then_inc(S("tiles"), 1)
            dve.wait_ge(S("base_ps"), nth("base_ps", L + 1))
            dve.tensor_scalar(base[:, 0:E], bank(1)[:, 0:E], float(P), 1.0, ALU.mult, ALU.add).then_inc(S("base"), 1)
            dve.wait_ge(S("end_ps"), nth("end_ps", L + 1))
            dve.tensor_copy(tiles_of[0:E, 2:3], bank(2)[0:E, 0:1]).then_inc(S("end"), 1)
            dve.wait_ge(S("end"), nth("end", L + 1))
            dve.tensor_scalar(ended[0:E, 0:NX], iota16[0:E, 0:NX], tiles_of[0:E, 2:3], None, ALU.is_ge).then_inc(S("ended"), 1)
            dve.wait_ge(S("base"), L + 1)
            dve.tensor_tensor(key, rank[:, :, 0:E], base[:, 0:E].unsqueeze(1).broadcast_to([P, NT, E]), ALU.add).then_inc(S("key_all"), 1)
            dve.wait_ge(S("key_all"), nth("key_all", L + 1))
            dve.tensor_tensor(key, key, sel[:, :, 0:E], ALU.mult).then_inc(S("key"), 1)
            dve.wait_ge(S("key"), nth("key", L + 1))
            if per == 1:
                dve.tensor_reduce(slots[:, 0:n], key, X_AXIS, ALU.max).then_inc(S("slots"), NT)
            else:
                for t in range(NT):
                    dve.max(slots[:, per * t:per * t + per], key[:, t, :]).then_inc(S("slots"), 1)
            dve.wait_ge(S("slots"), NT * (L + 1))
            dve.tensor_scalar(slot_i[:, 0:n], slots[:, 0:n], -1.0, None, ALU.add).then_inc(S("slot_i"), 1)
            dve.wait_ge(S("slot_i"), nth("slot_i", L + 1))
            dve.tensor_scalar(tmp_i[:, 0:n], slot_i[:, 0:n], 7, None, ALU.arith_shift_right).then_inc(S("hi_i"), 1)
            dve.wait_ge(S("hi_i"), nth("hi_i", L + 1))
            dve.tensor_copy(slot_hi[:, 0:n], tmp_i[:, 0:n]).then_inc(S("hi"), 1)
            dve.wait_ge(S("hi"), nth("hi", L + 1))
            dve.tensor_scalar(slot_lo[:, 0:n], slot_hi[:, 0:n], -float(P), -1.0, ALU.mult, ALU.add).then_inc(S("lo_"), 1)
            dve.wait_ge(S("lo_"), nth("lo_", L + 1))
            dve.tensor_tensor(slot_lo[:, 0:n], slots[:, 0:n], slot_lo[:, 0:n], ALU.add).then_inc(S("lo"), 1)
            dve.wait_ge(S("lo"), nth("lo", L + 1))

            def pair4(i, t=None):
                for k in range(4):
                    m = 4 * i + k
                    if some(NT * L + m - 3):
                        dve.wait_ge(S("pair"), NT * L + m - 3)
                    dve.tensor_scalar(one_lo[:, k, :], iota16[:, 0:P], slot_lo[:, bass.ts(m, 1)], None, ALU.is_equal).then_inc(S("one_lo"), 1)
                    tok = token_id[:, bass.ts(m if t is None else t, 1)]
                    dve.tensor_scalar(one_hi[:, k, 0:NX], iota16[:, 0:NX], slot_hi[:, bass.ts(m, 1)], tok, ALU.is_equal, ALU.mult).then_inc(S("one_hi"), 1)
            if per == 1:
                pair4(0)
                with dve.Fori(1, n // 4, 1) as i:
                    pair4(i)
            else:
                def tile8(t):
                    pair4(2 * t, t)
                    pair4(2 * t + 1, t)
                tile8(0)
                with dve.Fori(1, NT, 1) as t:
                    tile8(t)
            dve.wait_ge(S("row_ps"), nth("row_ps", L + 1))
            dve.tensor_scalar(expert_of[:, 0:NX], bank(3)[0:1, 0:NX], float(E - 1), None, ALU.min).then_inc(S("expert_row"), 1)
            if some(NT * L + n):
                dve.wait_ge(S("pair"), NT * L + n)
            dve.tensor_copy(token_of[:, 0:NX], bank(4)[:, 0:NX]).then_inc(S("table"), 1)

        @block.tensor
        def _(pe):
            pe.wait_ge(S("ctx_in"), 16 * (NB + 6))
            for b in range(NB):
                for m in range(KC):
                    for c in range(KC):
                        i = pe.matmul(bank(2 * b + m)[:, 0:S2], wk[:, c, m * P:(m + 1) * P], cT[:, b, c, :], start=(c == 0), stop=(c == KC - 1))
                    i.then_inc(S("kT_ps"), 1)
            for b in range(NB):
                pe.wait_ge(S("kT"), KC * (b + 1))
                for m in range(KC):
                    for c in range(KC):
                        i = pe.matmul(bank(4 + 2 * b + m)[:, 0:S2], wq[:, c, m * P:(m + 1) * P], kT[:, b, c, :], start=(c == 0), stop=(c == KC - 1))
                    i.then_inc(S("qk_ps"), 1)
            for b in range(NB):
                for c in range(KC):
                    i = pe.matmul(bank(b)[0:1, 0:S2], bqc[:, c:c + 1], kT[:, b, c, :], start=(c == 0), stop=(c == KC - 1))
                i.then_inc(S("bqk_ps"), 1)
            for b in range(NB):
                for c in range(KC):
                    i = pe.matmul(bank(2 + b)[:, 0:D], cT[:, b, c, 0:P], wv[:, c, :], start=(c == 0), stop=(c == KC - 1))
                i.then_inc(S("v_ps"), 1)
            pe.wait_ge(S("qk"), NB * KC)
            for b in range(NB):
                for c in range(KC):
                    i = pe.matmul(bank(4 + b)[0:SL, 0:D], cT[:, b, c, P:S2], wv[:, c, :], start=(c == 0), stop=(c == KC - 1))
                i.then_inc(S("v_ps"), 1)

            def xn1_T(u):
                pe.wait_ge(S("xn1"), u + 1)
                if some(u):
                    pe.wait_ge(S("xn1T"), u)
                for c in range(KC):
                    i = pe.transpose(bank(0)[:, c * P:(c + 1) * P], xn1[:, c * P:(c + 1) * P], ident[:, :])
                i.then_inc(S("xn1T_ps"), 1)

            def scores0(u, b):
                pe.wait_ge(S("xn1T"), u + 1)
                if some(u):
                    pe.wait_ge(S("s0"), nth("s0", u))
                for c in range(KC):
                    pe.matmul(bank(1)[:, 0:S2], xn1T[:, c, :], qk[:, b, c, :], start=(c == 0), stop=False)
                pe.matmul(bank(1)[:, 0:S2], ones_row[:, :], bqk[0:1, b, :], start=False, stop=True).then_inc(S("s0_ps"), 1)

            def probs0_T(u):
                pe.wait_ge(S("p0"), u + 1)
                if some(u):
                    pe.wait_ge(S("p0T"), u)
                for c in range(2):
                    i = pe.transpose(bank(2)[:, c * P:(c + 1) * P], p0[:, c, :], ident[:, :])
                i.then_inc(S("p0T_ps"), 1)

            def attend0(u, b):
                pe.wait_ge(S("p0T"), u + 1)
                if some(u):
                    pe.wait_ge(S("x1"), nth("x1", u))
                for c in range(2):
                    i = pe.matmul(bank(3)[:, 0:D], p0T[:, c, :], v0[:, b, c, :], start=(c == 0), stop=(c == 1))
                i.then_inc(S("attn0_ps"), 1)

            def xn2_T(u):
                pe.wait_ge(S("xn2"), nth("xn2", u + 1))
                if some(u):
                    pe.wait_ge(S("xn2T"), u)
                for c in range(KC):
                    i = pe.transpose(bank(4)[:, c * P:(c + 1) * P], xn2[:, c * P:(c + 1) * P], ident[:, :])
                i.then_inc(S("xn2T_ps"), 1)

            def logits0(t):
                pe.wait_ge(S("xn2T"), t + 1)
                if some(t):
                    pe.wait_ge(S("x1s"), t)
                for c in range(KC):
                    i = pe.matmul(bank(7)[:, 0:E0], xn2T[:, c, :], wr[:, c, :], start=(c == 0), stop=(c == KC - 1))
                i.then_inc(S("lg0_ps"), 1)

            def hidden0(t, w, b, name):
                if some(t):
                    pe.wait_ge(S("h0"), nth("h0", t))
                for f in range(FC0):
                    for c in range(KC):
                        i = pe.matmul(bank(b)[:, f * P:(f + 1) * P], w[:, c, f * P:(f + 1) * P], xn2T[:, c, :], start=(c == 0), stop=(c == KC - 1))
                i.then_inc(S(name), 1)

            def ranks0(t):
                pe.wait_ge(S("sel0"), nth("sel0", t + 1))
                if some(t):
                    pe.wait_ge(S("sel_sum0"), nth("sel_sum0", t))
                pe.matmul(bank(7)[:, 0:E0], tri[:, :], row(sel, t)[:, 0:E0], start=True, stop=False)
                pe.matmul(bank(7)[:, 0:E0], ones16[:, :], sel_sum[:, 0:E0], start=False, stop=True).then_inc(S("rank0_ps"), 1)

            def down0(t):
                pe.wait_ge(S("h0"), nth("h0", t + 1))
                pe.wait_ge(S("rank0"), nth("rank0", t + 1))
                for f in range(FC0):
                    i = pe.matmul(bank(7)[:, 0:D], h0[:, f, :], wd[:, f, :], start=(f == 0), stop=(f == FC0 - 1))
                i.then_inc(S("ffn0_ps"), 1)

            pe.wait_ge(S("v0"), 2 * NB)
            pe.wait_ge(S("bqk"), NB)
            pe.wait_ge(S("ffn0_in"), 16 * 4)
            xn1_T(0)
            scores0(0, 0)
            probs0_T(0)
            attend0(0, 0)
            xn2_T(0)

            def ffn_then_next(t, b):
                xn1_T(t + 1)
                logits0(t)
                scores0(t + 1, b)
                hidden0(t, wg, 5, "gate0_ps")
                probs0_T(t + 1)
                hidden0(t, wu, 6, "up0_ps")
                attend0(t + 1, b)
                ranks0(t)
                down0(t)
                xn2_T(t + 1)
            ffn_then_next(0, 0)
            for b in range(NB):
                with pe.Fori(max(1, b * TPB - 1), (b + 1) * TPB - 1, 1) as t:
                    ffn_then_next(t, b)
            logits0(NT - 1)
            hidden0(NT - 1, wg, 5, "gate0_ps")
            hidden0(NT - 1, wu, 6, "up0_ps")
            ranks0(NT - 1)
            down0(NT - 1)

            pe.wait_ge(S("x1s"), NT)
            route_tensor(pe, one_lo0, one_hi0, E0, NX0, NT, 0)

            pe.wait_ge(S("fm_row"), 1)
            pe.matmul(bank(5)[:, 0:1], fmr[0:1, :], ones_row[0:1, 0:1], start=True, stop=True).then_inc(S("fmc_ps"), 1)
            pe.wait_ge(S("cL"), NB * KC)
            pe.wait_ge(S("fmc"), 1)
            for b in range(NB):
                if some(NG * HG * b):
                    pe.wait_ge(S("kbd"), NG * HG * b)
                for g in range(NG):
                    i = pe.matmul(bank(5 + g // 2)[:, (g % 2) * S2:(g % 2 + 1) * S2], fm2[:, g % 2, :], cT[:, b, g // 2, :], start=True, stop=True)
                i.then_inc(S("kf_ps"), 1)
                if some(b):
                    pe.wait_ge(S("vb"), b)
                for g in range(NG):
                    pe.matmul(bank(7)[:, g * P:(g + 1) * P], cT[:, b, g // 2, 0:P], fm2[:, g % 2, :], start=True, stop=False)
                    i = pe.matmul(bank(7)[:, g * P:(g + 1) * P], ones_row[:, :], fmr[0:1, :], start=False, stop=True)
                i.then_inc(S("vf_ps"), 1)
                if some(b):
                    pe.wait_ge(S("vl"), b)
                pe.wait_ge(S("base"), 1)
                for g in range(NG):
                    pe.matmul(bank(1)[0:SL * HG, g * P:(g + 1) * P], cL[:, b, g // 2, :], fm2[:, g % 2, :], start=True, stop=False)
                    i = pe.matmul(bank(1)[0:SL * HG, g * P:(g + 1) * P], ones_row[:, 0:SL * HG], fmr[0:1, :], start=False, stop=True)
                i.then_inc(S("vl_ps"), 1)

            def x0_T(n, k):
                j = n * RING + k
                p = k % 2
                pe.wait_ge(S(f"rows_in{k}"), 16 * (n + 1))
                if some(j - 1):
                    pe.wait_ge(S("x0T"), j - 1)
                for c in range(KC):
                    i = pe.transpose(bank(4 + p)[:, c * P:(c + 1) * P], g0[:, k, c * P:(c + 1) * P], ident[:, :])
                i.then_inc(S("x0T_ps"), 1)

            def gate_up0(n, k):
                j = n * RING + k
                p = k % 2
                pe.wait_ge(S(f"gu_in{p}"), 16 * (n * (RING // 2) + k // 2 + 1))
                pe.wait_ge(S("x0T"), j + 1)
                if some(j - 1):
                    pe.wait_ge(S("e0T"), j - 1)
                for half in range(2):
                    for f in range(FC0):
                        for c in range(KC):
                            at = half * F0 + f * P
                            i = pe.matmul(bank(2 * half + p)[:, f * P:(f + 1) * P], expert_gu[p][:, c, at:at + P], x0T[:, p, c, :], start=(c == 0), stop=(c == KC - 1))
                    i.then_inc(S("eg0_ps" if half == 0 else "eu0_ps"), 1)

            def expert_down0(n, k):
                j = n * RING + k
                p = k % 2
                pe.wait_ge(S(f"dn_in{p}"), 16 * (n * (RING // 2) + k // 2 + 1))
                pe.wait_ge(S("e0T"), j + 1)
                if some(j - 1):
                    pe.wait_ge(S("y0"), j - 1)
                for f in range(FC0):
                    i = pe.matmul(bank(6 + p)[:, 0:D], e0T[:, p, f, :], expert_dn[p][:, f, :], start=(f == 0), stop=(f == FC0 - 1))
                i.then_inc(S("dn0"), 1)

            def experts0(n):
                for k in range(RING):
                    gate_up0(n, k)
                    if k + 1 < RING:
                        x0_T(n, k + 1)
                    elif not (isinstance(n, int) and n == GROUPS0 - 1):
                        x0_T(n + 1, 0)
                    if k > 0:
                        expert_down0(n, k - 1)
                    elif not (isinstance(n, int) and n == 0):
                        expert_down0(n - 1, RING - 1)
            pe.wait_ge(S("table"), 1)
            pe.wait_ge(S("expert_row"), 1)
            pe.wait_ge(S("setup1_done"), 1)
            x0_T(0, 0)
            group_loop(pe, GROUPS0, experts0)
            expert_down0(GROUPS0 - 1, RING - 1)

            pe.wait_ge(S("y0"), NX0)
            pe.wait_ge(S("small1_in"), 16 * 6)

            def xn3_T(u):
                pe.wait_ge(S("xn3"), nth("xn3", u + 1))
                for c in range(KC):
                    i = pe.transpose(bank(7)[:, c * P:(c + 1) * P], xn3[:, c * P:(c + 1) * P], ident[:, :])
                i.then_inc(S("xn3T_ps"), 1)

            def features(u):
                pe.wait_ge(S("xn3T"), u + 1)
                for g in range(NG):
                    i = pe.matmul(bank(7)[:, g * P:(g + 1) * P], fm2[:, g % 2, :], xn3T[:, g // 2, :], start=True, stop=True)
                i.then_inc(S("qf_ps"), 1)

            def scores1(t, g, b):
                s = 2 * (g % 2)
                pe.wait_ge(S("qf"), t + 1)
                if some(NG * t + g - 1):
                    pe.wait_ge(S("prob"), NG * t + g - 1)
                for h in range(HG):
                    i = pe.matmul(bank(s + h // 2)[:, (h % 2) * S2:(h % 2 + 1) * S2], qf[:, g, :], kbd[:, b, HG * g + h, :], start=True, stop=True)
                i.then_inc(S("s1_ps"), 1)

            def probs1_T(t, g):
                p = g % 2
                pe.wait_ge(S("prob"), NG * t + g + 1)
                if some(NG * t + g):
                    pe.wait_ge(S("probT"), NG * t + g)
                if g == 0:
                    if some(t):
                        pe.wait_ge(S("ofT"), t)
                for h in range(HG):
                    i = pe.transpose(bank(4)[:, h * P:(h + 1) * P], prob[:, p].rearrange("p (k h) -> p h k", h=HG)[:, h, 0:P], ident[:, :])
                i.then_inc(S("probT_ps"), 1)
                if some(NG * t + g):
                    pe.wait_ge(S("leftT"), NG * t + g)
                pe.transpose(bank(5)[0:SL * HG, 0:P], prob[:, p, P * HG:S2 * HG], ident[:, :]).then_inc(S("leftT_ps"), 1)

            def attend1(t, g, b):
                p = g % 2
                pe.wait_ge(S("leftT"), NG * t + g + 1)
                pe.wait_ge(S("probT"), NG * t + g + 1)
                if g % 2 == 0:
                    if some((NG // 2) * t + g // 2):
                        pe.wait_ge(S("of"), (NG // 2) * t + g // 2)
                o = bank(6)[:, p * HG * VW:(p + 1) * HG * VW]
                pe.matmul(o, leftT[0:SL * HG, p, :], vl[0:SL * HG, b, HG * g:HG * (g + 1), :].rearrange("p h v -> p (h v)"), start=True, stop=True)
                for h in range(HG):
                    i = pe.matmul(o[:, h * VW:(h + 1) * VW], probT[:, p, h, :], vb[:, b, HG * g + h, :], start=False, stop=True, skip_group_check=True)
                i.then_inc(S("o_ps"), 1)

            def of_T(t):
                pe.wait_ge(S("of"), (NG // 2) * (t + 1))
                pe.wait_ge(S("probT"), NG * (t + 1))
                for g in range(NG):
                    i = pe.transpose(bank(4)[:, g * P:(g + 1) * P], of[:, HG * g:HG * (g + 1), :].rearrange("p h f -> p (h f)"), ident[:, :])
                i.then_inc(S("ofT_ps"), 1)

            def project(t):
                pe.wait_ge(S("ofT"), t + 1)
                for g in range(NG):
                    i = pe.matmul(bank(7)[:, 0:D], ofT[:, g, :], fcw[:, g, :], start=(g == 0), stop=(g == NG - 1))
                i.then_inc(S("fc_ps"), 1)

            def xn4_T(t):
                pe.wait_ge(S("xn4"), nth("xn4", t + 1))
                for c in range(KC):
                    i = pe.transpose(bank(7)[:, c * P:(c + 1) * P], xn4[:, c * P:(c + 1) * P], ident[:, :])
                i.then_inc(S("xn4T_ps"), 1)

            def logits1(t):
                pe.wait_ge(S("xn4T"), t + 1)
                for c in range(KC):
                    pe.matmul(bank(7)[:, 0:E1], xn4T[:, c, :], cen[:, c, :], start=(c == 0), stop=(c == KC - 1))
                for c in range(KC):
                    i = pe.matmul(bank(7)[:, E1:E1 + P], wsu[:, c, :], xn4T[:, c, :], start=(c == 0), stop=(c == KC - 1))
                i.then_inc(S("lg1_ps"), 1)

            def shared1(t):
                pe.wait_ge(S("hs1"), nth("hs1", t + 1))
                pe.wait_ge(S("aff"), nth("aff", t + 1))
                pe.matmul(bank(7)[:, 0:D], hs1T, wsd, start=True, stop=True).then_inc(S("ffn1_ps"), 1)

            def ranks1(t):
                pe.wait_ge(S("sel1"), nth("sel1", t + 1))
                if some(t):
                    pe.wait_ge(S("sel_sum1"), nth("sel_sum1", t))
                pe.wait_ge(S("x3s"), t + 1)
                pe.matmul(bank(7)[:, 0:E1], tri[:, :], row(sel, t), start=True, stop=False)
                pe.matmul(bank(7)[:, 0:E1], ones16[:, :], sel_sum[:, :], start=False, stop=True).then_inc(S("rank1_ps"), 1)

            def last(t):
                return isinstance(t, int) and t == NT - 1

            def first(t):
                return isinstance(t, int) and t == 0

            def attention1(t, b):
                scores1(t, 0, b)
                scores1(t, 1, b)
                if not first(t):
                    of_T(t - 1)
                probs1_T(t, 0)
                if not first(t):
                    project(t - 1)
                scores1(t, 2, b)
                attend1(t, 0, b)
                probs1_T(t, 1)
                scores1(t, 3, b)
                if not first(t):
                    xn4_T(t - 1)
                attend1(t, 1, b)
                if not first(t):
                    logits1(t - 1)
                probs1_T(t, 2)
                if not first(t):
                    shared1(t - 1)
                attend1(t, 2, b)
                if not first(t):
                    ranks1(t - 1)
                probs1_T(t, 3)
                if not last(t):
                    if some(t):
                        pe.wait_ge(S("rank1"), nth("rank1", t))
                    xn3_T(t + 1)
                attend1(t, 3, b)
                if not last(t):
                    features(t + 1)

            start_ahead(pe, "projection1_psum")
            xn3_T(0)
            features(0)
            attention1(0, 0)
            with pe.Fori(1, TPB, 1) as t:
                attention1(t, 0)
            with pe.Fori(TPB, NT - 1, 1) as t:
                attention1(t, NB - 1)
            attention1(NT - 1, NB - 1)
            t = NT - 1
            of_T(t)
            project(t)
            xn4_T(t)
            logits1(t)
            shared1(t)
            ranks1(t)
            pe.wait_ge(S("rank1"), nth("rank1", NT))
            route_tensor(pe, one_lo1, one_hi1, E1, NX1, NT * TOP1, 1)

            def x1_T(n, k):
                j = n * RING + k
                p = k % 2
                pe.wait_ge(S(f"rows_in{k}"), 16 * (n + 1 + GROUPS0))
                if some(j - 1):
                    pe.wait_ge(S("x1T"), j - 1)
                for c in range(KC):
                    i = pe.transpose(bank(p)[:, c * P:(c + 1) * P], g1[:, k, c * P:(c + 1) * P], ident[:, :])
                i.then_inc(S("x1T_ps"), 1)

            def up1(n, k):
                j = n * RING + k
                p = k % 2
                pe.wait_ge(S("x1T"), j + 1)
                if some(j - 1):
                    pe.wait_ge(S("h1"), j - 1)
                pe.sem_inc(S("waited_pe"), 1)
                e = pe.value_load(expert_of[0:1, bass.ts(j, 1)], min_val=0, max_val=E1 - 1)
                for c in range(KC):
                    i = pe.matmul(bank(2 + p)[:, 0:F1], x1T[:, p, c, :], w_up1[:, bass.ts(e, 1), c, :], start=(c == 0), stop=(c == KC - 1))
                i.then_inc(S("up1_ps"), 1)

            def h1_T(n, k):
                j = n * RING + k
                p = k % 2
                pe.wait_ge(S("h1"), j + 1)
                if some(j - 1):
                    pe.wait_ge(S("h1T"), j - 1)
                pe.transpose(bank(4 + p)[:, 0:P], h1[:, p, :], ident[:, :]).then_inc(S("h1T_ps"), 1)

            def down1(n, k):
                j = n * RING + k
                p = k % 2
                pe.wait_ge(S("h1T"), j + 1)
                if some(j - 1):
                    pe.wait_ge(S("y1"), j - 1)
                pe.sem_inc(S("waited_pe"), 1)
                e = pe.value_load(expert_of[0:1, bass.ts(j, 1)], min_val=0, max_val=E1 - 1)
                pe.matmul(bank(6 + p)[:, 0:D], h1T[:, p, :], w_dn1[:, bass.ts(e, 1), :], start=True, stop=True).then_inc(S("dn1_ps"), 1)

            def lag(step, n, k, d):
                k -= d
                if k < 0:
                    if not (isinstance(n, int) and n == 0):
                        step(n - 1, k + RING)
                elif k >= RING:
                    if not (isinstance(n, int) and n == GROUPS1 - 1):
                        step(n + 1, k - RING)
                else:
                    step(n, k)

            def experts1(n):
                for k in range(RING):
                    lag(up1, n, k, 0)
                    lag(x1_T, n, k, -1)
                    lag(h1_T, n, k, 1)
                    lag(down1, n, k, 2)
            pe.wait_ge(S("w1_in"), 16 * (E1 // 8) * (KC + 1))
            pe.wait_ge(S("table"), 2)
            pe.wait_ge(S("expert_row"), 2)
            x1_T(0, 0)
            group_loop(pe, GROUPS1, experts1)
            n = GROUPS1 - 1
            h1_T(n, RING - 1)
            down1(n, RING - 2)
            down1(n, RING - 1)


        @block.scalar
        def _(act):
            for i in range(4):
                n = NT // 4
                act.dma_start(X[:, n * i:n * i + n, :], x_t[:, n * i:n * i + n, :]).then_inc(S("x_in"), 16)
            for b in range(NB):
                for m in range(KC):
                    act.wait_ge(S("qk_ps"), KC * b + m + 1)
                    act.activation(qk[:, b, m, :], bank(4 + 2 * b + m)[:, 0:S2], ACT.Copy, scale=QS).then_inc(S("qk"), 1)
            for b in range(NB):
                act.wait_ge(S("bqk_ps"), b + 1)
                act.activation(bqk[0:1, b, :], bank(b)[0:1, 0:S2], ACT.Copy, scale=QS).then_inc(S("bqk"), 1)

            def xn1_T(u):
                act.wait_ge(S("xn1T_ps"), nth("xn1T_ps", u + 1))
                if some(u):
                    act.wait_ge(S("s0_ps"), nth("s0_ps", u))
                act.activation(xn1T.rearrange("p c n -> p (c n)"), bank(0)[:, 0:D], ACT.Copy).then_inc(S("xn1T"), 1)

            def probs0(u):
                act.wait_ge(S("nm0"), nth("nm0", u + 1))
                if some(u):
                    act.wait_ge(S("p0T_ps"), nth("p0T_ps", u))
                if some(u):
                    act.wait_ge(S("rinv0"), nth("rinv0", u))
                act.activation(p0.rearrange("p c n -> p (c n)")[:, 0:S2], s0, ACT.Exp, bias=nm0[:, :], accum_out=rsum[:, :]).then_inc(S("p0"), 1)

            def probs0_T(u):
                act.wait_ge(S("p0T_ps"), nth("p0T_ps", u + 1))
                if some(u):
                    act.wait_ge(S("attn0_ps"), nth("attn0_ps", u))
                act.activation(p0T.rearrange("p c n -> p (c n)"), bank(2)[:, 0:2 * P], ACT.Copy).then_inc(S("p0T"), 1)

            def xn2_T(u):
                act.wait_ge(S("xn2T_ps"), nth("xn2T_ps", u + 1))
                if some(u):
                    act.wait_ge(S("up0_ps"), nth("up0_ps", u))
                act.activation(xn2T.rearrange("p c n -> p (c n)"), bank(4)[:, 0:D], ACT.Copy).then_inc(S("xn2T"), 1)

            def score0(t):
                act.wait_ge(S("best0"), nth("best0", t + 1))
                if some(t):
                    act.wait_ge(S("score0"), nth("score0", t))
                act.activation(sg_e[:, 0:1], best[:, 0:1], ACT.Exp, scale=-1.0).then_inc(S("sg0"), 1)

            def gate0(t):
                act.wait_ge(S("gate0_ps"), nth("gate0_ps", t + 1))
                if some(t):
                    act.wait_ge(S("ha0"), nth("ha0", t))
                act.activation(th0, bank(5), ACT.Tanh, scale=0.5).then_inc(S("th0"), 1)

            xn1_T(0)
            probs0(0)
            probs0_T(0)
            xn2_T(0)

            def ffn_then_next(t):
                xn1_T(t + 1)
                score0(t)
                probs0(t + 1)
                gate0(t)
                probs0_T(t + 1)
                xn2_T(t + 1)
            ffn_then_next(0)
            with act.Fori(1, NT - 1, 1) as t:
                ffn_then_next(t)
            score0(NT - 1)
            gate0(NT - 1)

            act.wait_ge(S("fmc_ps"), 1)
            act.activation(fmc, bank(5)[:, 0:1], ACT.Copy).then_inc(S("fmc"), 1)
            act.wait_ge(S("fmc"), 1)
            act.wait_ge(S("setup1_zeroed"), 1)
            for b in range(NB):
                act.wait_ge(S("kf_ps"), b + 1)
                for g in range(NG):
                    for h in range(HG):
                        rows = slice(FD * h, FD * h + FD)
                        act.activation(kbd[rows, b, HG * g + h, :], bank(5 + g // 2)[rows, (g % 2) * S2:(g % 2 + 1) * S2], ACT.Exp,
                                       bias=fmc[rows, :]).then_inc(S("kbd"), 1)
                act.wait_ge(S("vf_ps"), b + 1)
                act.activation(vb[:, b, :, 0:FD], bank(7).rearrange("p (h f) -> p h f", h=NH), ACT.Exp).then_inc(S("vb"), 1)
                act.wait_ge(S("vl_ps"), b + 1)
                act.activation(vl[0:SL * HG, b, :, 0:FD], bank(1)[0:SL * HG, :].rearrange("p (h f) -> p h f", h=NH), ACT.Exp).then_inc(S("vl"), 1)

            def x0_T(n, k):
                j = n * RING + k
                act.wait_ge(S("x0T_ps"), j + 1)
                if some(j - 1):
                    act.wait_ge(S("eu0_ps"), j - 1)
                act.activation(x0T[:, k % 2].rearrange("p c n -> p (c n)"), bank(4 + k % 2)[:, 0:D], ACT.Copy).then_inc(S("x0T"), 1)

            def silu0(n, k):
                j = n * RING + k
                act.wait_ge(S("eg0_ps"), j + 1)
                if some(j - 1):
                    act.wait_ge(S("e0T"), j - 1)
                act.activation(sg0[:, k % 2], bank(k % 2), ACT.Silu).then_inc(S("sg0x"), 1)

            def experts0(n):
                for k in range(RING):
                    silu0(n, k)
                    if k + 1 < RING:
                        x0_T(n, k + 1)
                    elif not (isinstance(n, int) and n == GROUPS0 - 1):
                        x0_T(n + 1, 0)
            x0_T(0, 0)
            group_loop(act, GROUPS0, experts0)

            def xn3_T(u):
                act.wait_ge(S("xn3T_ps"), nth("xn3T_ps", u + 1))
                act.activation(xn3T.rearrange("p c n -> p (c n)"), bank(7)[:, 0:D], ACT.Copy).then_inc(S("xn3T"), 1)

            def features(u):
                act.wait_ge(S("qf_ps"), nth("qf_ps", u + 1))
                act.activation(qf.rearrange("p g n -> p (g n)"), bank(7), ACT.Exp, bias=fmc).then_inc(S("qf"), 1)

            def probs1(t, g):
                act.wait_ge(S("nmax"), NG * t + g + 1)
                if some(NG * t + g - 1):
                    act.wait_ge(S("leftT_ps"), NG * t + g - 1)
                for h in range(HG):
                    src = bank(2 * (g % 2) + h // 2)[:, (h % 2) * S2:(h % 2 + 1) * S2]
                    i = act.activation(prob[:, g % 2].rearrange("p (k h) -> p h k", h=HG)[:, h, :], src, ACT.Exp, bias=nmax2[:, g % 2, h:h + 1])
                i.then_inc(S("prob"), 1)

            def probs1_T(t, g):
                act.wait_ge(S("leftT_ps"), NG * t + g + 1)
                if some(NG * t + g - 1):
                    act.wait_ge(S("o_ps"), NG * t + g - 1)
                act.activation(leftT[0:SL * HG, g % 2], bank(5)[0:SL * HG, 0:P], ACT.Copy).then_inc(S("leftT"), 1)

            def xn4_T(t):
                act.wait_ge(S("xn4T_ps"), nth("xn4T_ps", t + 1))
                act.activation(xn4T.rearrange("p c n -> p (c n)"), bank(7)[:, 0:D], ACT.Copy).then_inc(S("xn4T"), 1)

            def logits1(t):
                act.wait_ge(S("lg1_ps"), nth("lg1_ps", t + 1))
                if some(t):
                    act.wait_ge(S("hs1"), nth("hs1", t))
                act.activation(th1, bank(7)[:, E1:E1 + P], ACT.Tanh, scale=0.5).then_inc(S("th1"), 1)
                if some(t):
                    act.wait_ge(S("w_sig"), nth("w_sig", t))
                act.wait_ge(S("aff"), nth("aff", t + 1))
                act.activation(sg_e[:, :], lg[:, :], ACT.Exp, scale=-1.0).then_inc(S("sg1"), 1)

            def last(t):
                return isinstance(t, int) and t == NT - 1

            def first(t):
                return isinstance(t, int) and t == 0

            def attention1(t):
                probs1(t, 0)
                probs1(t, 1)
                probs1_T(t, 0)
                probs1(t, 2)
                probs1_T(t, 1)
                if not first(t):
                    xn4_T(t - 1)
                probs1(t, 3)
                if not first(t):
                    logits1(t - 1)
                probs1_T(t, 2)
                probs1_T(t, 3)
                if not last(t):
                    xn3_T(t + 1)
                    features(t + 1)
            xn3_T(0)
            features(0)
            tile_loop(act, attention1)
            xn4_T(NT - 1)
            logits1(NT - 1)

            def x1_T(n, k):
                j = n * RING + k
                act.wait_ge(S("x1T_ps"), j + 1)
                if some(j - 1):
                    act.wait_ge(S("up1_ps"), j - 1)
                act.activation(x1T[:, k % 2].rearrange("p c n -> p (c n)"), bank(k % 2)[:, 0:D], ACT.Copy).then_inc(S("x1T"), 1)

            def silu1(n, k):
                j = n * RING + k
                act.wait_ge(S("up1_ps"), j + 1)
                if some(j - 1):
                    act.wait_ge(S("h1T_ps"), j - 1)
                act.activation(h1[:, k % 2, :], bank(2 + k % 2)[:, 0:F1], ACT.Silu).then_inc(S("h1"), 1)

            def experts1(n):
                for k in range(RING):
                    silu1(n, k)
                    if k + 1 < RING:
                        x1_T(n, k + 1)
                    elif not (isinstance(n, int) and n == GROUPS1 - 1):
                        x1_T(n + 1, 0)
            x1_T(0, 0)
            group_loop(act, GROUPS1, experts1)

        @block.vector
        def _(dve):
            dve.memset(ones16[:, :], 1.0).then_inc(S("dve_const"), 1)
            dve.memset(ones_row[:, :], 1.0).then_inc(S("dve_const"), 1)
            dve.memset(neg_half[:, :], -0.5).then_inc(S("neg_half"), 1)
            dve.memset(fm2, 0.0).then_inc(S("zeroed"), 1)
            dve.memset(p0, 0.0).then_inc(S("dve_const"), 1)
            dve.memset(v0[:, :, 1, :], 0.0).then_inc(S("dve_const"), 1)
            dve.memset(sel_sum[:, :], 0.0).then_inc(S("dve_const"), 1)
            dve.memset(kbd, 0.0).then_inc(S("dve_zero1"), 1)
            dve.memset(vl[:, :, :, FD:VW], 1.0).then_inc(S("dve_zero1"), 1)
            dve.memset(vb[:, :, :, FD:VW], 1.0).then_inc(S("dve_zero1"), 1)
            dve.wait_ge(S("dve_zero1"), 3)
            dve.sem_inc(S("setup1_zeroed"), 1)

            dve.wait_ge(S("dve_const"), 5)
            dve.wait_ge(S("ctx_in"), 16 * (NB + 6))
            for b in range(NB):
                for m in range(KC):
                    dve.wait_ge(S("kT_ps"), KC * b + m + 1)
                    dve.tensor_scalar(kT[:, b, m, :], bank(2 * b + m)[:, 0:S2], bkc[:, m:m + 1], None, ALU.add).then_inc(S("kT"), 1)
            dve.wait_ge(S("x_in"), 64)

            for t in range(NT):
                dve.bn_stats(weight[:, t, 0:6], X[:, t, :]).then_inc(S("stats1"), 1)
            for t in range(NT):
                dve.wait_ge(S("stats1"), t + 1)
                dve.bn_aggr(mv_all[:, t, :], weight[:, t, 0:6]).then_inc(S("mv1"), 1)
            dve.wait_ge(S("mv1"), NT)
            dve.tensor_scalar(rstd_all[:, :], mv_all[:, :, 1], LN_EPS, None, ALU.add).then_inc(S("var1"), 1)
            for b in range(NB):
                dve.wait_ge(S("v_ps"), b + 1)
                dve.tensor_tensor(v0[:, b, 0, :], bank(2 + b)[:, 0:D], bvb, ALU.add).then_inc(S("v0"), 1)
            for b in range(NB):
                dve.wait_ge(S("v_ps"), NB + b + 1)
                dve.tensor_tensor(v0[0:SL, b, 1, :], bank(4 + b)[0:SL, 0:D], bvb[0:SL, :], ALU.add).then_inc(S("v0"), 1)
            dve.wait_ge(S("rstd1"), 1)
            dve.wait_ge(S("mask_in"), 16)

            def norm1(u):
                if some(u):
                    dve.wait_ge(S("xn1T_ps"), nth("xn1T_ps", u))
                dve.tensor_scalar(xn1, row(X, u), row(mv_all, u)[:, 0:1], rstd_all[:, bass.ts(u, 1)], ALU.subtract, ALU.mult).then_inc(S("xn1"), 1)

            def softmax0(u, m):
                dve.wait_ge(S("s0_ps"), nth("s0_ps", u + 1))
                if some(u):
                    dve.wait_ge(S("p0"), u)
                dve.scalar_tensor_tensor(s0, row(msk, m), MASKED, bank(1)[:, 0:S2], ALU.mult, ALU.add).then_inc(S("s0"), 1)
                dve.wait_ge(S("s0"), nth("s0", u + 1))
                dve.tensor_reduce(nm0[:, :], s0, X_AXIS, ALU.max, negate=True).then_inc(S("nm0"), 1)

            def residual1(u):
                dve.wait_ge(S("p0"), u + 1)
                dve.reciprocal(rinv[:, :], rsum[:, :]).then_inc(S("rinv0"), 1)
                dve.wait_ge(S("attn0_ps"), nth("attn0_ps", u + 1))
                dve.wait_ge(S("rinv0"), nth("rinv0", u + 1))
                dve.scalar_tensor_tensor(row(X, u), bank(3)[:, 0:D], rinv[:, :], row(X, u), ALU.mult, ALU.add).then_inc(S("x1"), 1)
                dve.wait_ge(S("x1"), nth("x1", u + 1))
                dve.sem_inc(S("waited_dve"), 1)
                norm(u, "2", xn2, (("xn2T_ps", u),))

            def norm(t, name, dst, free):
                dve.bn_stats(stats[:, :], row(X, t)).then_inc(S("stats" + name), 1)
                dve.wait_ge(S("stats" + name), nth("stats" + name, t + 1))
                dve.sem_inc(S("waited_dve"), 1)
                dve.bn_aggr(mv[:, :], stats[:, :]).then_inc(S("mv" + name), 1)
                dve.wait_ge(S("mv" + name), nth("mv" + name, t + 1))
                dve.tensor_scalar(var_eps[:, :], mv[:, 1:2], LN_EPS, None, ALU.add).then_inc(S("var" + name), 1)
                dve.wait_ge(S("rstd" + name), t + 1)
                for product, n in free:
                    if some(n):
                        dve.wait_ge(S(product), n)
                dve.tensor_scalar(dst, row(X, t), mv[:, 0:1], rstd[:, :], ALU.subtract, ALU.mult).then_inc(S("xn" + name), 1)

            def router0(t):
                dve.wait_ge(S("lg0_ps"), nth("lg0_ps", t + 1))
                if some(t):
                    dve.wait_ge(S("sel0"), nth("sel0", t))
                dve.tensor_copy(lg[:, 0:E0], bank(7)[:, 0:E0]).then_inc(S("lg0"), 1)
                dve.wait_ge(S("lg0"), nth("lg0", t + 1))
                if some(t):
                    dve.wait_ge(S("sg0"), t)
                dve.sem_inc(S("waited_dve"), 1)
                dve.max(best[:, :], lg[:, 0:E0]).then_inc(S("best0"), 1)
                dve.wait_ge(S("best0"), nth("best0", t + 1))
                dve.sem_inc(S("waited_dve"), 1)
                dve.max_index(best_i[:, :], best[:, :], lg[:, 0:E0]).then_inc(S("best_i0"), 1)
                dve.wait_ge(S("best_i0"), nth("best_i0", t + 1))
                dve.tensor_copy(small[:, 0:1], best_i[:, 0:1]).then_inc(S("top0"), 1)
                dve.wait_ge(S("top0"), nth("top0", t + 1))
                dve.tensor_scalar(row(sel, t)[:, 0:E0], iota16[:, 0:E0], small[:, 0:1], None, ALU.is_equal).then_inc(S("sel0"), 1)
                dve.wait_ge(S("sg0"), t + 1)
                dve.tensor_scalar(sg_d[:, 0:1], sg_e[:, 0:1], 1.0, None, ALU.add).then_inc(S("sgd0"), 1)
                dve.wait_ge(S("sgd0"), nth("sgd0", t + 1))
                dve.reciprocal(sg_d[:, 1:2], sg_d[:, 0:1]).then_inc(S("score0"), 1)
                dve.wait_ge(S("score0"), nth("score0", t + 1))
                if some(t * 16):
                    dve.wait_ge(S("xs0_stored"), t * 16)
                dve.tensor_scalar(xs0, xn2, sg_d[:, 1:2], None, ALU.mult).then_inc(S("xs0"), 1)

            def ranks0(t):
                dve.wait_ge(S("rank0_ps"), nth("rank0_ps", t + 1))
                dve.tensor_copy(row(rank, t)[:, 0:E0], bank(7)[:, 0:E0]).then_inc(S("rank0"), 1)
                dve.tensor_tensor(sel_sum[:, 0:E0], sel_sum[:, 0:E0], row(sel, t)[:, 0:E0], ALU.add).then_inc(S("sel_sum0"), 1)

            def hidden0(t):
                dve.wait_ge(S("th0"), t + 1)
                dve.scalar_tensor_tensor(a0, th0, 1.0, bank(5), ALU.add, ALU.mult).then_inc(S("ha0"), 1)
                dve.wait_ge(S("ha0"), nth("ha0", t + 1))
                dve.wait_ge(S("up0_ps"), nth("up0_ps", t + 1))
                if some(t):
                    dve.wait_ge(S("ffn0_ps"), nth("ffn0_ps", t))
                dve.scalar_tensor_tensor(h0.rearrange("p c n -> p (c n)"), a0, 0.5, bank(6), ALU.mult, ALU.mult).then_inc(S("h0"), 1)

            def shared0(t):
                dve.wait_ge(S("ffn0_ps"), nth("ffn0_ps", t + 1))
                dve.tensor_tensor(row(X, t), row(X, t), bank(7)[:, 0:D], ALU.add).then_inc(S("x1s"), 1)

            norm1(0)
            softmax0(0, 0)
            residual1(0)
            norm1(1)

            def ffn_then_next(t, m, more):
                router0(t)
                softmax0(t + 1, m)
                hidden0(t)
                residual1(t + 1)
                ranks0(t)
                shared0(t)
                if more:
                    norm1(t + 2)
            dve.wait_ge(S("consts"), 1)
            dve.tensor_reduce(head_of[:, :], head_at, X_AXIS, ALU.add).then_inc(S("head_of"), 1)
            ffn_then_next(0, 1, True)
            with dve.Fori(1, TPB - 1, 1) as t:
                ffn_then_next(t, t + 1, True)
            with dve.Fori(TPB - 1, NT - 2, 1) as t:
                ffn_then_next(t, t + 1 - TPB, True)
            ffn_then_next(NT - 2, TPB - 1, False)
            router0(NT - 1)
            hidden0(NT - 1)
            ranks0(NT - 1)
            dve.wait_ge(S("sel_sum0"), nth("sel_sum0", NT))
            dve.sem_inc(S("sel_total"), 1)
            shared0(NT - 1)

            dve.wait_ge(S("fm_in"), 16 * 2 * (P // HD))
            fmv = fm2.rearrange("p a (h s e) -> p a h s e", s=2, e=HD)
            for a in range(2):
                i = dve.tensor_scalar(fmv[:, a, :, 1, :], fmv[:, a, :, 0, :], -1.0, None, ALU.mult)
            fmrv = fmr[0:1, :].rearrange("p (h s e) -> p h s e", s=2, e=HD)
            dve.tensor_scalar(fmrv[:, :, 1, :], fmrv[:, :, 1, :], -1.0, None, ALU.mult).then_inc(S("fm_row"), 1)
            for b in range(NB):
                for c in range(KC):
                    dst = cL[:, b, c, :].rearrange("p (k h) -> p k h", h=HG)
                    dve.tensor_copy(dst, cT[:, b, c, P:S2].unsqueeze(2).broadcast_to([P, SL, HG])).then_inc(S("cL"), 1)

            route_vector(dve, key0, one_lo0, one_hi0, E0, NX0, 1, 0)
            dve.wait_ge(S("kbd"), NB * NG * HG)
            dve.tensor_scalar(kbd, kbd, QS, None, ALU.mult).then_inc(S("kbd_scaled"), 1)
            dve.wait_ge(S("kbd_scaled"), 1)
            dve.wait_ge(S("vb"), NB)
            for b in range(NB):
                dve.wait_ge(S("vl"), b + 1)
                for h in range(HG):
                    dve.wait_ge(S("head_of"), 1)
                    own = vl[0:SL * HG, b, :, :].rearrange("p (g h) v -> p g h v", h=HG)[:, :, h, :]
                    dve.tensor_scalar(own, own, head_of[0:SL * HG, h:h + 1], None, ALU.mult).then_inc(S("vl_own"), 1)
            dve.wait_ge(S("vl_own"), NB * HG)
            dve.sem_inc(S("setup1_done"), 1)

            def hidden_x0(n, k):
                j = n * RING + k
                p = k % 2
                dve.wait_ge(S("sg0x"), j + 1)
                dve.wait_ge(S("eu0_ps"), j + 1)
                if some(j - 1):
                    dve.wait_ge(S("dn0"), j - 1)
                dve.tensor_tensor(e0T[:, p].rearrange("p c n -> p (c n)"), sg0[:, p], bank(2 + p), ALU.mult).then_inc(S("e0T"), 1)

            def out_x0(n, k):
                j = n * RING + k
                dve.wait_ge(S("dn0"), j + 1)
                if some(16 * n):
                    dve.wait_ge(S(f"rows_out{k}"), 16 * n)
                dve.tensor_copy(y0[:, k], bank(6 + k % 2)[:, 0:D]).then_inc(S("y0"), 1)

            def experts0(n):
                for k in range(RING):
                    hidden_x0(n, k)
                    if k > 0:
                        out_x0(n, k - 1)
                    elif not (isinstance(n, int) and n == 0):
                        out_x0(n - 1, RING - 1)
            group_loop(dve, GROUPS0, experts0)
            out_x0(GROUPS0 - 1, RING - 1)

            def residual2(u):
                dve.wait_ge(S("yg"), 16 * (u + 1))
                dve.tensor_tensor(row(X, u), row(X, u), yg, ALU.add).then_inc(S("x2"), 1)
                dve.wait_ge(S("x2"), nth("x2", u + 1))
                dve.sem_inc(S("waited_dve"), 1)
                norm(u, "3", xn3, (("xn3T_ps", u),))
                dve.wait_ge(S("xn3"), nth("xn3", u + 1))
                dve.tensor_tensor(row(X, u), row(X, u), fcb, ALU.add).then_inc(S("x2b"), 1)

            def softmax1(t, g):
                dve.wait_ge(S("s1_ps"), NG * t + g + 1)
                if some(NG * t + g - 1):
                    dve.wait_ge(S("prob"), NG * t + g - 1)
                src = PS[:, 2 * (g % 2):2 * (g % 2) + 2, 0:2 * S2].rearrange("p b (h k) -> p b h k", h=2)
                dve.tensor_reduce(nmax2[:, g % 2, :].rearrange("p (b h) -> p b h", b=2), src, X_AXIS, ALU.max, negate=True).then_inc(S("nmax"), 1)

            def probs1_T(t, g):
                dve.wait_ge(S("probT_ps"), NG * t + g + 1)
                if some(NG * t + g - 1):
                    dve.wait_ge(S("o_ps"), NG * t + g - 1)
                dve.tensor_copy(probT[:, g % 2].rearrange("p h n -> p (h n)"), bank(4)).then_inc(S("probT"), 1)

            def heads(t, g):
                half = g // 2
                dve.wait_ge(S("o_ps"), NG * t + g + 1)
                if some((NG // 2) * t + half):
                    dve.wait_ge(S("of"), (NG // 2) * t + half)
                o = bank(6)[:, 0:2 * HG * VW].rearrange("p (h v) -> p h v", v=VW)
                dve.reciprocal(den[:, :], o[:, :, FD]).then_inc(S("den"), 1)
                dve.wait_ge(S("den"), (NG // 2) * t + half + 1)
                if half == 0:
                    if some(t):
                        dve.wait_ge(S("ofT_ps"), nth("ofT_ps", t))
                dve.tensor_tensor(of[:, 2 * HG * half:2 * HG * (half + 1), :], o[:, :, 0:FD], den[:, :].unsqueeze(2).broadcast_to([P, 2 * HG, FD]), ALU.mult).then_inc(S("of"), 1)

            def of_T(t):
                dve.wait_ge(S("ofT_ps"), nth("ofT_ps", t + 1))
                if some(t):
                    dve.wait_ge(S("fc_ps"), nth("fc_ps", t))
                dve.tensor_copy(ofT.rearrange("p g n -> p (g n)"), bank(4)).then_inc(S("ofT"), 1)

            def residual3(t):
                dve.wait_ge(S("fc_ps"), nth("fc_ps", t + 1))
                dve.wait_ge(S("x2b"), nth("x2b", t + 1))
                dve.tensor_tensor(row(X, t), row(X, t), bank(7)[:, 0:D], ALU.add).then_inc(S("x3"), 1)
                dve.wait_ge(S("x3"), nth("x3", t + 1))
                dve.sem_inc(S("waited_dve"), 1)
                norm(t, "4", xn4, (("xn4T_ps", t), ("xn4_stored", t * 16)))

            def router1(t):
                dve.wait_ge(S("lg1_ps"), nth("lg1_ps", t + 1))
                if some(t):
                    dve.wait_ge(S("sg1"), t)
                if some(t):
                    dve.wait_ge(S("rep1"), nth("rep1", t))
                dve.wait_ge(S("th1"), t + 1)
                dve.tensor_copy(lg[:, :], bank(7)[:, 0:E1]).then_inc(S("aff"), 1)
                if some(t):
                    dve.wait_ge(S("ffn1_ps"), nth("ffn1_ps", t))
                dve.scalar_tensor_tensor(hs1T, th1, 1.0, bank(7)[:, E1:E1 + P], ALU.add, ALU.mult).then_inc(S("hs1"), 1)
                dve.wait_ge(S("aff"), nth("aff", t + 1))
                dve.tensor_tensor(lg2[:, :], lg[:, :], ebb, ALU.add).then_inc(S("biased"), 1)
                dve.wait_ge(S("biased"), nth("biased", t + 1))
                dve.sem_inc(S("waited_dve"), 1)
                dve.max(best[:, :], lg2[:, :]).then_inc(S("best1"), 1)
                dve.wait_ge(S("best1"), nth("best1", t + 1))
                dve.sem_inc(S("waited_dve"), 1)
                dve.match_replace(small[:, :], best[:, :], lg2[:, :], -3.0e38).then_inc(S("rep1"), 1)
                dve.wait_ge(S("rep1"), nth("rep1", t + 1))
                dve.tensor_tensor(row(sel, t), small[:, :], lg2[:, :], ALU.not_equal).then_inc(S("sel1"), 1)

            def shared1(t):
                dve.wait_ge(S("ffn1_ps"), nth("ffn1_ps", t + 1))
                dve.scalar_tensor_tensor(row(X, t), bank(7)[:, 0:D], 0.5, row(X, t), ALU.mult, ALU.add).then_inc(S("x3s"), 1)

            def weights1(t):
                dve.wait_ge(S("sg1"), t + 1)
                dve.tensor_scalar(sg_d[:, :], sg_e[:, :], 1.0, None, ALU.add).then_inc(S("w_sig"), 1)
                dve.wait_ge(S("w_sig"), nth("w_sig", t + 1))
                dve.reciprocal(lg2[:, :], sg_d[:, :]).then_inc(S("w_rec"), 1)
                dve.wait_ge(S("w_rec"), nth("w_rec", t + 1))
                dve.scalar_tensor_tensor(row(weight, t), lg2[:, :], 1.0, row(sel, t), ALU.mult, ALU.mult, accum_out=wsum[:, 0:1]).then_inc(S("w_sum"), 1)
                dve.wait_ge(S("w_sum"), nth("w_sum", t + 1))
                dve.tensor_scalar(wsum[:, 0:1], wsum[:, 0:1], 1e-8, None, ALU.add).then_inc(S("w_sume"), 1)
                dve.wait_ge(S("w_sume"), nth("w_sume", t + 1))
                dve.reciprocal(wsum[:, 1:2], wsum[:, 0:1]).then_inc(S("w_inv"), 1)
                dve.wait_ge(S("w_inv"), nth("w_inv", t + 1))
                dve.tensor_scalar(row(weight, t), row(weight, t), wsum[:, 1:2], None, ALU.mult).then_inc(S("weight"), 1)

            def ranks1(t):
                dve.wait_ge(S("rank1_ps"), nth("rank1_ps", t + 1))
                dve.tensor_copy(row(rank, t), bank(7)[:, 0:E1]).then_inc(S("rank1"), 1)
                dve.tensor_tensor(sel_sum[:, :], sel_sum[:, :], row(sel, t), ALU.add).then_inc(S("sel_sum1"), 1)

            def last(t):
                return isinstance(t, int) and t == NT - 1

            def first(t):
                return isinstance(t, int) and t == 0

            def attention1(t):
                softmax1(t, 0)
                softmax1(t, 1)
                if not first(t):
                    of_T(t - 1)
                probs1_T(t, 0)
                if not first(t):
                    residual3(t - 1)
                softmax1(t, 2)
                probs1_T(t, 1)
                softmax1(t, 3)
                heads(t, 1)
                if not first(t):
                    router1(t - 1)
                probs1_T(t, 2)
                if not first(t):
                    shared1(t - 1)
                    weights1(t - 1)
                    ranks1(t - 1)
                if not last(t):
                    residual2(t + 1)
                probs1_T(t, 3)
                heads(t, 3)

            dve.wait_ge(S("small1_in"), 16 * 6)
            dve.memset(sel_sum[:, :], 0.0).then_inc(S("sums_zeroed"), 1)
            dve.wait_ge(S("sums_zeroed"), 1)
            start_ahead(dve, "router1_steps")
            start_ahead(dve, "weights1_steps")
            residual2(0)
            tile_loop(dve, attention1)
            t = NT - 1
            of_T(t)
            residual3(t)
            router1(t)
            shared1(t)
            weights1(t)
            ranks1(t)
            dve.wait_ge(S("sel_sum1"), nth("sel_sum1", NT))
            dve.wait_ge(S("x3s"), NT)
            dve.sem_inc(S("attention1_done"), 1)
            dve.wait_ge(S("xn4_stored"), 16 * NT)
            dve.sem_inc(S("sel_total"), 1)

            route_vector(dve, slot_key, one_lo1, one_hi1, E1, NX1, TOP1, 1)

            def h1_T(n, k):
                j = n * RING + k
                p = k % 2
                dve.wait_ge(S("h1T_ps"), j + 1)
                if some(j - 1):
                    dve.wait_ge(S("dn1_ps"), j - 1)
                dve.tensor_copy(h1T[:, p, :], bank(4 + p)[:, 0:P]).then_inc(S("h1T"), 1)

            def out_x1(n, k):
                j = n * RING + k
                dve.wait_ge(S("dn1_ps"), j + 1)
                dve.wait_ge(S(f"rows_out{k}"), 16 * (n + GROUPS0))
                dve.tensor_copy(y1[:, k], bank(6 + k % 2)[:, 0:D]).then_inc(S("y1"), 1)

            def lag(step, n, k, d):
                k -= d
                if k >= 0:
                    step(n, k)
                elif not (isinstance(n, int) and n == 0):
                    step(n - 1, k + RING)

            def experts1(n):
                for k in range(RING):
                    lag(h1_T, n, k, 1)
                    lag(out_x1, n, k, 2)
            group_loop(dve, GROUPS1, experts1)
            n = GROUPS1 - 1
            h1_T(n, RING - 1)
            out_x1(n, RING - 2)
            out_x1(n, RING - 1)

            def slot_weights(t):
                for k in range(TOP1):
                    m = t * TOP1 + k
                    dve.scalar_tensor_tensor(slot_junk[:, k, :], row(slot_key, t), slots[:, bass.ts(m, 1)], row(weight, t), ALU.is_equal, ALU.mult,
                                             accum_out=w_slot[:, bass.ts(m, 1)]).then_inc(S("w_slot"), 1)
            for t in range(NT):
                if t:
                    if some(TOP1 * t):
                        dve.wait_ge(S("w_slot"), TOP1 * t)
                slot_weights(t)
            dve.wait_ge(S("w_slot"), NT * TOP1)

            def combine(i):
                for half in range(2):
                    t = i * 2 + half
                    for k in range(TOP1):
                        if some(16 * (i + 1 + (1 - half) * (GROUPS0 + GROUPS1))):
                            dve.wait_ge(S(f"rows_in{RING * half + k}"), 16 * (i + 1 + (1 - half) * (GROUPS0 + GROUPS1)))
                        if some(TOP1 * t + k):
                            dve.wait_ge(S("acc"), TOP1 * t + k)
                        ins = dve.scalar_tensor_tensor(row(X, t), cg[:, half, k, :], w_slot[:, bass.ts(t * TOP1 + k, 1)], row(X, t), ALU.mult, ALU.add)
                        ins.then_inc(S("acc"), 1)
                    dve.wait_ge(S("acc"), TOP1 * (t + 1))
                    dve.sem_inc(S("final"), 1)
            combine(0)
            with dve.Fori(1, NT // 2, 1) as i:
                combine(i)

        @block.gpsimd
        def _(pool):
            pool.memset(ident[:, :], 0.0).then_inc(S("pool_const"), 1)
            pool.memset(tri[:, :], 0.0).then_inc(S("pool_const"), 1)
            pool.memset(triinc[:, :], 0.0).then_inc(S("pool_const"), 1)
            pool.memset(head_at, 0.0).then_inc(S("pool_const"), 1)
            pool.wait_ge(S("pool_const"), 4)
            pool.affine_select(out=head_at, in_=head_at, compare_op=ALU.not_equal, fill=1.0, base=0, pattern=[[-1, HG], [-HG, SL]], channel_multiplier=1).then_inc(S("pool_const"), 1)
            pool.affine_select(out=ident[:, :], in_=ident[:, :], compare_op=ALU.not_equal, fill=1.0, base=0, pattern=[[-1, P]], channel_multiplier=1).then_inc(S("pool_const"), 1)
            pool.affine_select(out=tri[:, :], in_=tri[:, :], compare_op=ALU.is_ge, fill=1.0, base=0, pattern=[[-1, P]], channel_multiplier=1).then_inc(S("pool_const"), 1)
            pool.affine_select(out=triinc[:, :], in_=triinc[:, :], compare_op=ALU.is_gt, fill=1.0, base=0, pattern=[[-1, P]], channel_multiplier=1).then_inc(S("pool_const"), 1)
            pool.iota(iota16[:, :], pattern=[[1, NX1]], base=0, channel_multiplier=0, allow_small_or_imprecise_dtypes=True).then_inc(S("pool_const"), 1)
            pool.iota(step128[:, :], pattern=[[P, NT]], base=0, channel_multiplier=0, allow_small_or_imprecise_dtypes=True).then_inc(S("pool_const"), 1)
            pool.iota(token_id[:, :], pattern=[[P, NT]], base=0, channel_multiplier=1, allow_small_or_imprecise_dtypes=True).then_inc(S("pool_const"), 1)
            pool.wait_ge(S("pool_const"), 11)
            pool.sem_inc(S("consts"), 1)
            pool.wait_ge(S("neg_half"), 1)
            pool.wait_ge(S("var1"), 1)
            pool.tensor_tensor(out=rstd_all[:, :], in0=rstd_all[:, :], in1=neg_half[:, :], op=ALU.pow).then_inc(S("rstd1"), 1)

            def power(name, t):
                pool.wait_ge(S("var" + name), nth("var" + name, t + 1))
                pool.tensor_tensor(out=rstd[:, :], in0=var_eps[:, :], in1=neg_half[:, 0:1], op=ALU.pow).then_inc(S("rstd" + name), 1)
            power("2", 0)
            with pool.Fori(1, NT, 1) as t:
                power("2", t)

            def gathers(i, L, src, dst, before):
                for s in range(2):
                    n = i * 2 + s
                    for k in range(RING):
                        if some(n * 16 + 16 * (before - 1)):
                            pool.wait_ge(S(f"rows_in{k}"), n * 16 + 16 * (before - 1))
                    pool.tensor_copy(idx8[:, s, :], token_of[:, bass.ts(n, RING)]).then_inc(S(f"idx{L}"), 1)
                    pool.wait_ge(S(f"idx{L}"), n + 1)
                    for k in range(RING):
                        if some(n * RING + k - RING + 1):
                            pool.wait_ge(S(f"x{L}T_ps"), n * RING + k - RING + 1)
                        pool.sem_inc(S("waited_pool"), 1)
                        pool.indirect_dma_start(out=dst[:, k, :], out_offset=None, in_=src,
                                                in_offset=bass.IndirectOffsetOnAxis(ap=idx8[:, s, k:k + 1], axis=0)).then_inc(S(f"rows_in{k}"), 16)
            pool.wait_ge(S("table"), 1)
            pool.wait_ge(S("xs0_stored"), 16 * NT)
            gathers(0, 0, scaled0, g0, 0)
            with pool.Fori(1, GROUPS0 // 2, 1) as i:
                gathers(i, 0, scaled0, g0, 0)

            for k in range(RING):
                pool.wait_ge(S(f"rows_out{k}"), 16 * GROUPS0)

            def gather_y0(u):
                if some(u):
                    pool.wait_ge(S("x2"), nth("x2", u))
                pool.tensor_copy(idx1[:, :], slot_i[:, bass.ts(u, 1)]).then_inc(S("idx_y"), 1)
                pool.wait_ge(S("idx_y"), u + 1)
                pool.sem_inc(S("waited_pool"), 1)
                pool.indirect_dma_start(out=yg, out_offset=None, in_=routed0, in_offset=bass.IndirectOffsetOnAxis(ap=idx1[:, 0:1], axis=0)).then_inc(S("yg"), 16)

            gather_y0(0)
            power("3", 0)
            gather_y0(1)
            def around(t):
                if not (isinstance(t, int) and t == 0):
                    power("4", t - 1)
                if not (isinstance(t, int) and t == NT - 1):
                    power("3", t + 1)
                    if not (isinstance(t, int) and t == NT - 2):
                        gather_y0(t + 2)
            around(0)
            with pool.Fori(1, NT - 2, 1) as t:
                around(t)
            around(NT - 2)
            around(NT - 1)
            power("4", NT - 1)

            pool.wait_ge(S("table"), 2)
            gathers(0, 1, normed1, g1, GROUPS0)
            with pool.Fori(1, GROUPS1 // 2, 1) as i:
                gathers(i, 1, normed1, g1, GROUPS0)

            def combine(i):
                for half in range(2):
                    t = i * 2 + half
                    if half == 0:
                        for h in range(2):
                            for k in range(TOP1):
                                if some(16 * (i + (1 - h) * (GROUPS0 + GROUPS1))):
                                    pool.wait_ge(S(f"rows_in{RING * h + k}"), 16 * (i + (1 - h) * (GROUPS0 + GROUPS1)))
                        pool.tensor_copy(idx8[:, :, :].rearrange("p a b -> p (a b)"), slot_i[:, bass.ts(i, 2 * TOP1)]).then_inc(S("idx_c"), 1)
                        pool.wait_ge(S("idx_c"), i + 1)
                    for k in range(TOP1):
                        if some(TOP1 * t + k - 2 * TOP1 + 1):
                            pool.wait_ge(S("acc"), TOP1 * t + k - 2 * TOP1 + 1)
                        pool.sem_inc(S("waited_pool"), 1)
                        pool.indirect_dma_start(out=cg[:, half, k, :], out_offset=None, in_=routed1,
                                                in_offset=bass.IndirectOffsetOnAxis(ap=idx8[:, half, k:k + 1], axis=0)).then_inc(S(f"rows_in{RING * half + k}"), 16)
            for k in range(RING):
                pool.wait_ge(S(f"rows_out{k}"), 16 * (GROUPS0 + GROUPS1))
            combine(0)
            with pool.Fori(1, NT // 2, 1) as i:
                combine(i)



_OUT = ((2, 1024, 256), "float32")


def _layout(inputs):
    import numpy as np
    a = {k: np.asarray(v) for k, v in inputs.items()}
    named = {
        "x": a["x"].reshape(-1, a["x"].shape[-1]),
        "ctxT": a["ctx_1024"].transpose(0, 2, 1),
        "mask": a["mask_SxS2_fk1"],
        "WqT": a["L0_xattn_Wq"].T, "bq": a["L0_xattn_bq"].reshape(-1, P).T,
        "Wk": a["L0_xattn_Wk"], "bk": a["L0_xattn_bk"].reshape(-1, P).T,
        "Wv": a["L0_xattn_Wv"], "bv": a["L0_xattn_bv"],
        "w_routerT": a["L0_ffn_w_router"].T,
        "gate_up": a["L0_ffn_gate_up_proj"], "down": a["L0_ffn_down_proj"],
        "w_gateT": a["L0_ffn_w_gate"].T, "w_upT": a["L0_ffn_w_up"].T, "w_downT": a["L0_ffn_w_down"].T,
        "fm_wT": a["L1_xattn_fm_w"].T, "fm_b": a["L1_xattn_fm_b"],
        "fc_wT": a["L1_xattn_fc_w"].T, "fc_b": a["L1_xattn_fc_b"],
        "centroidsT": a["L1_ffn_centroids"].T, "expert_biases": a["L1_ffn_expert_biases"],
        "Ws_up": a["L1_ffn_Ws_up"], "Ws_down": a["L1_ffn_Ws_down"],
        "W_up": a["L1_ffn_W_up"], "W_down": a["L1_ffn_W_down"],
    }
    return {k: np.ascontiguousarray(v) for k, v in named.items()}


def kernel(**inputs):
    import concourse.bacc as bacc
    from concourse.bass_utils import run_bass_kernel_spmd as run

    nc = bacc.Bacc("TRN2", target_bir_lowering=False, num_devices=1)
    arrays, args = {}, {}
    for name, a in _layout(inputs).items():
        arrays[f"in_{name}"] = a
        args[name] = nc.dram_tensor(f"in_{name}", a.shape, mybir.dt.from_np(a.dtype), kind="ExternalInput").ap()
    result = nc.dram_tensor("out_x", [_OUT[0][0] * _OUT[0][1], _OUT[0][2]], F32, kind="ExternalOutput").ap()
    build(nc, **args, out=result)
    r = run(nc, [arrays], core_ids=[0])
    return r.results[0]["out_x"].reshape(_OUT[0])
```

```python
import math
from contextlib import ExitStack

import concourse.bass as bass
from concourse import mybir

F32 = mybir.dt.float32
F16 = mybir.dt.float16
I32 = mybir.dt.int32
U32 = mybir.dt.uint32
ALU = mybir.AluOpType
ACT = mybir.ActivationFunctionType
X_AXIS = mybir.AxisListType.X

P = 128
BANK = 512
LN_EPS = 1e-5
MASKED = -1000000000.0


def build(nc, x, ctxT, mask, WqT, bq, Wk, bk, Wv, bv, w_routerT, gate_up, down, w_gateT, w_upT, w_downT,
          fm_wT, fm_b, fc_wT, fc_b, centroidsT, expert_biases, Ws_up, Ws_down, W_up, W_down, out):
    TOK, D = x.shape
    NB, _, S2 = ctxT.shape
    NT = TOK // P
    TPB = NT // NB
    KC = D // P
    SL = S2 - P
    QS = float(D) ** -0.5
    E0, _, F2 = gate_up.shape
    F0 = F2 // 2
    FC0 = F0 // P
    E1, _, F1 = W_up.shape
    TOP1 = 8
    HD = fm_b.shape[0]
    NH = D // HD
    FD = 2 * HD
    HG = P // FD
    NG = NH // HG
    VW = FD + 1
    NX0 = 32
    NX1 = 192
    assert NX0 >= E0 - 1 + TOK // P and NX1 >= E1 - 1 + TOK * TOP1 // P
    RING = 8
    GROUPS0, GROUPS1 = NX0 // RING, NX1 // RING

    scaled0 = nc.dram_tensor("scaled0", [TOK, D], F32).ap()
    routed0 = nc.dram_tensor("routed0", [NX0 * P, D], F32).ap()
    normed1 = nc.dram_tensor("normed1", [TOK, D], F32).ap()
    routed1 = nc.dram_tensor("routed1", [NX1 * P, D], F32).ap()

    ctx = ExitStack()
    with ctx:
        def sb(name, shape, dt=F32):
            return ctx.enter_context(nc.sbuf_tensor(name, shape, dt))

        sems = {}

        STEPS = {}
        for shared, names in (
            ("attention0_psum", ("xn1T_ps", "s0_ps", "p0T_ps", "attn0_ps")),
            ("ffn0_psum", ("lg0_ps", "gate0_ps", "rank0_ps", "up0_ps", "ffn0_ps")),
            ("attention0_sbuf", ("xn1T", "p0", "p0T")),
            ("ffn0_sbuf", ("sg0", "th0")),
            ("softmax0_steps", ("s0", "nm0", "rinv0")),
            ("norm2_steps", ("x1", "stats2", "mv2", "var2", "xn2")),
            ("router0_steps", ("lg0", "best0", "best_i0", "top0", "sel0", "sgd0", "score0", "xs0")),
            ("hidden0_steps", ("ha0", "h0")),
            ("counts0_steps", ("rank0", "sel_sum0")),
            ("projection1_psum", ("ofT_ps", "fc_ps", "xn4T_ps", "lg1_ps", "ffn1_ps", "rank1_ps")),
            ("query1_psum", ("xn3T_ps", "qf_ps")),
            ("norm3_steps", ("x2", "stats3", "mv3", "var3", "xn3", "x2b")),
            ("norm4_steps", ("x3", "stats4", "mv4", "var4", "xn4")),
            ("router1_steps", ("hs1", "biased", "best1", "rep1", "sel1")),
            ("weights1_steps", ("w_exp1", "w_sig", "w_sel", "w_sum", "w_sume", "w_inv", "weight")),
            ("counts1_steps", ("rank1", "sel_sum1")),
            ("route_psum", ("count_ps", "base_ps", "end_ps", "row_ps")),
            ("route_steps", ("count", "ntiles", "end", "key_all", "key", "slot_i", "hi_i", "hi", "lo_", "lo")),
        ):
            for i, name in enumerate(names):
                STEPS[name] = (shared, i + 1, len(names))

        def S(name):
            name = STEPS[name][0] if name in STEPS else name
            if name not in sems:
                sems[name] = ctx.enter_context(nc.semaphore(name))
            return sems[name]

        def nth(name, n):
            if name not in STEPS:
                return n
            _, step, steps = STEPS[name]
            return n * steps + (step - steps)

        def some(n):
            return not (isinstance(n, int) and n <= 0)


        X = sb("X", [P, NT, D])
        ident = sb("ident", [P, P])
        tri = sb("tri", [P, P], F16)
        triinc = sb("triinc", [P, P], F16)
        ones16 = sb("ones16", [P, P], F16)
        ones_row = sb("ones_row", [1, P])
        iota16 = sb("iota16", [P, NX1], F16)
        step128 = sb("step128", [P, NT])
        token_id = sb("token_id", [P, NT])
        neg_half = sb("neg_half", [P, NT])
        stats = sb("stats", [P, 6])
        mv_all = sb("mv_all", [P, NT, 2])
        rstd_all = sb("rstd_all", [P, NT])
        mv = sb("mv", [P, 2])
        var_eps = sb("var_eps", [P, 1])
        rstd = sb("rstd", [P, 1])
        small = sb("small", [P, 64])
        rank = sb("rank", [P, NT, E1])
        sel = sb("sel", [P, NT, E1], F16)
        weight = sb("weight", [P, NT, E1])
        sel_sum = sb("sel_sum", [P, E1], F16)
        tiles_of = sb("tiles_of", [P, 4])
        tiles16 = sb("tiles16", [P, 1 + P], F16)
        ended = sb("ended", [P, NX1], F16)
        base = sb("base", [P, E1])
        slots = sb("slots", [P, NT * TOP1])
        slot_i = sb("slot_i", [P, NT * TOP1], I32)
        tmp_i = sb("tmp_i", [P, NT * TOP1], I32)
        slot_hi = sb("slot_hi", [P, NT * TOP1])
        slot_lo = sb("slot_lo", [P, NT * TOP1])
        w_slot = sb("w_slot", [P, NT * TOP1])
        token_of = sb("token_of", [P, NX1], I32)
        expert_of = sb("expert_of", [1, NX1], I32)
        idx8 = sb("idx8", [P, 2, RING], I32)
        idx1 = sb("idx1", [P, 1], I32)
        head_of = sb("head_of", [P, HG])
        log_scale = sb("log_scale", [P, 1])
        one_col = sb("one_col", [P, 1])

        den = sb("den", [P, 2 * HG])
        lg = sb("lg", [P, E1])
        lg2 = sb("lg2", [P, E1])
        best = sb("best", [P, 8])
        best_i = sb("best_i", [P, 8], U32)
        rsum = sb("rsum", [P, 1])
        rinv = sb("rinv", [P, 1])
        nm0 = sb("nm0", [P, 1])
        sg_e = sb("sg_e", [P, E1])
        sg_d = sb("sg_d", [P, E1])
        wsum = sb("wsum", [P, 2])
        nmax2 = sb("nmax2", [P, 2, HG])

        R = sb("R", [P, E1 * KC * P + E1 * D])
        Q = sb("Q", [P, 11204])

        def carver(region, at=0):
            where = [at]

            def take(*dims):
                n = 1
                for d in dims:
                    n *= d
                v = region[:, where[0]:where[0] + n]
                where[0] += n
                if len(dims) == 2:
                    v = v.rearrange("p (a b) -> p a b", a=dims[0])
                if len(dims) == 3:
                    v = v.rearrange("p (a b c) -> p a b c", a=dims[0], b=dims[1])
                if len(dims) == 4:
                    v = v.rearrange("p (a b c d) -> p a b c d", a=dims[0], b=dims[1], c=dims[2])
                return v
            return take

        r = carver(R)
        WB = 4
        ffn_at = WB * (KC * F2 + FC0 * D) - (2 * KC * F0 + FC0 * D)
        expert_w = [(r(KC, F2), r(FC0, D)) for _ in range(WB)]
        r = carver(R, ffn_at)
        wg, wu, wd = r(KC, F0), r(KC, F0), r(FC0, D)
        wr = r(KC, E0)
        cT = r(NB, KC, S2)
        cL = r(NB, KC, SL * HG)
        wk, wq, wv = r(KC, D), r(KC, D), r(KC, D)
        bkc, bqc, bvb = r(KC), r(KC), r(D)
        kT = r(NB, KC, S2)
        qk = r(NB, KC, S2)
        bqk = r(NB, S2)
        v0 = r(NB, 2, D)
        msk = r(TPB, S2)
        xn1, xn1T, s0, p0, p0T = r(D), r(KC, P), r(S2), r(2, P), r(2, P)
        xn2, xn2T, xs0 = r(D), r(KC, P), r(D)
        th0, a0, h0 = r(F0), r(F0), r(FC0, P)
        g0, y0 = r(RING, D), r(RING, D)
        x0T, sg0, e0T = r(2, KC, P), r(2, F0), r(2, FC0, P)
        key0 = r(NT, E0)
        head_at = r(HG, SL)
        one_lo0 = r(4 * P // 2).bitcast(F16).rearrange("p (k n) -> p k n", k=4)
        one_hi0 = r(4 * NX0 // 2).bitcast(F16).rearrange("p (k n) -> p k n", k=4)

        NUP = E1 * KC * F1
        w_up1 = R[:, 0:NUP].rearrange("p (e c f) -> p e c f", e=E1, c=KC)
        w_dn1 = R[:, NUP:NUP + E1 * D].rearrange("p (e d) -> p e d", e=E1)
        LATE = 24
        r = carver(R, NUP + (E1 - LATE) * D)
        prob = r(2, S2 * HG)
        probT, leftT = r(2, HG, P), r(2, P)
        of, ofT = r(NH, FD), r(NG, P)
        th1, hs1T = r(P), r(P)
        q = carver(Q)
        kbd, vb, vl = q(NB, NH, S2), q(NB, NH, VW), q(NB, NH, VW)
        fcw, wsu, wsd, cen = q(NG, D), q(KC, F1), q(D), q(KC, E1)
        fcb, ebb = q(D), q(E1)
        fm2, fmr, fmc, fmk = q(2, P), q(P), q(1), q(1)
        yg, xn3, xn3T, qf = q(D), q(D), q(KC, P), q(NG, P)
        xn4, xn4T = q(D), q(KC, P)
        q = carver(Q)
        g1, y1 = q(RING, D), q(RING, D)
        x1T, h1, h1T = q(2, KC, P), q(2, F1), q(2, P)
        cg = q(2, TOP1, D)
        slot_key = q(NT, E1)
        slot_junk = q(TOP1, E1)
        q = carver(Q)
        one_lo1 = q(4 * P // 2).bitcast(F16).rearrange("p (k n) -> p k n", k=4)
        one_hi1 = q(4 * NX1 // 2).bitcast(F16).rearrange("p (k n) -> p k n", k=4)
        away = q(2 * P // 2).bitcast(F16).rearrange("p (k n) -> p k n", k=2)

        PS = ctx.enter_context(nc.psum_tensor("PS", [P, 8, BANK], F32))

        def bank(b):
            return PS[:, b, :]

        x_t = x.rearrange("(t p) d -> p t d", p=P)
        out_t = out.rearrange("(t p) d -> t p d", p=P)
        block = ctx.enter_context(nc.Block())

        def chunks(a):
            return a.rearrange("(c p) n -> p c n", p=P)

        def tile_loop(eng, body):
            body(0)
            with eng.Fori(1, NT - 1, 1) as t:
                body(t)
            body(NT - 1)

        def group_loop(eng, groups, body):
            body(0)
            with eng.Fori(1, groups - 1, 1) as n:
                body(n)
            body(groups - 1)

        def row(ap, t):
            return ap[:, bass.ts(t, 1), :].rearrange("p a d -> p (a d)")

        @block.sync
        def _(sp):
            for b in range(NB):
                sp.dma_start(cT[:, b], chunks(ctxT[b])).then_inc(S("ctx_in"), 16)
            for dst, src in ((wk, Wk), (wq, WqT), (wv, Wv)):
                sp.dma_start(dst, chunks(src)).then_inc(S("ctx_in"), 16)
            sp.dma_start(bkc, bk).then_inc(S("ctx_in"), 16)
            sp.dma_start(bqc, bq).then_inc(S("ctx_in"), 16)
            sp.dma_start(bvb, bv.partition_broadcast(P)).then_inc(S("ctx_in"), 16)
            sp.dma_start(msk, mask.rearrange("(t p) k -> p t k", p=P)).then_inc(S("mask_in"), 16)
            for dst, src in ((wr, w_routerT), (wg, w_gateT), (wu, w_upT), (wd, w_downT)):
                sp.dma_start(dst, chunks(src)).then_inc(S("ffn0_in"), 16)
            for dst, src in ((fcw, fc_wT), (wsu, Ws_up), (cen, centroidsT)):
                sp.dma_start(dst, chunks(src)).then_inc(S("small1_in"), 16)
            sp.dma_start(wsd, Ws_down).then_inc(S("small1_in"), 16)
            sp.dma_start(fcb, fc_b.partition_broadcast(P)).then_inc(S("small1_in"), 16)
            sp.dma_start(ebb, expert_biases.partition_broadcast(P)).then_inc(S("small1_in"), 16)
            sp.wait_ge(S("zeroed"), 1)
            for h in range(P // HD):
                dst = fm2[HD * h:HD * h + HD, h // HG, FD * (h % HG):FD * (h % HG) + HD]
                sp.dma_start(dst, fm_wT).then_inc(S("fm_in"), 16)
                sp.dma_start(fmr[0:1, HD * h:HD * h + HD], fm_b.rearrange("(a e) -> a e", a=1)).then_inc(S("fm_in"), 16)

            def store0(t):
                sp.wait_ge(S("xs0"), nth("xs0", t + 1))
                sp.dma_start(scaled0[bass.ts(t, P), :], xs0).then_inc(S("xs0_stored"), 16)
            store0(0)
            with sp.Fori(1, NT, 1) as t:
                store0(t)

            sp.wait_ge(S("expert_row"), 1)

            def load0(n, k):
                j = n * RING + k
                if some(j - WB + 1):
                    sp.wait_ge(S("dn0"), j - WB + 1)
                e = sp.value_load(expert_of[0:1, bass.ts(j, 1)], min_val=0, max_val=E0 - 1)
                gu, dn = expert_w[k % WB]
                sp.dma_start(gu, gate_up[bass.ts(e, 1), :, :].rearrange("a (c p) f -> p (a c) f", p=P)).then_inc(S(f"w0_in{k % WB}"), 16)
                sp.dma_start(dn, down[bass.ts(e, 1), :, :].rearrange("a (c p) f -> p (a c) f", p=P)).then_inc(S(f"w0_in{k % WB}"), 16)

            def out0(n, k):
                sp.wait_ge(S("y0"), n * RING + k + 1)
                sp.dma_start(routed0[bass.ts(n * RING + k, P), :], y0[:, k]).then_inc(S(f"rows_out{k}"), 16)

            def experts0(n):
                for k in range(RING):
                    load0(n, k)
                    if k >= WB:
                        out0(n, k - WB)
                    elif not (isinstance(n, int) and n == 0):
                        out0(n - 1, k + RING - WB)
            group_loop(sp, GROUPS0, experts0)
            for k in range(RING - WB, RING):
                out0(GROUPS0 - 1, k)

            sp.wait_ge(S("y0"), NX0)
            for k in range(RING):
                sp.wait_ge(S(f"rows_out{k}"), 16 * GROUPS0)
            sp.wait_ge(S("setup1_done"), 1)
            EB = 8

            def store1(t):
                sp.wait_ge(S("xn4"), nth("xn4", t + 1))
                sp.dma_start(normed1[bass.ts(t, P), :], xn4).then_inc(S("xn4_stored"), 16)
            ups, downs = E1 // EB, (E1 - LATE) // EB
            with sp.Fori(0, ups, 1) as t:
                store1(t)
                for c in range(KC):
                    sp.dma_start(w_up1[:, bass.ts(t, EB), c], W_up[bass.ts(t, EB), c * P:(c + 1) * P].rearrange("e p f -> p e f")).then_inc(S("w1_in"), 16)
            with sp.Fori(0, downs, 1) as i:
                store1(i + ups)
                sp.dma_start(w_dn1[:, bass.ts(i, EB)], W_down[bass.ts(i, EB)].rearrange("e f d -> f e d")).then_inc(S("w1_in"), 16)
            with sp.Fori(ups + downs, NT, 1) as t:
                store1(t)
            sp.wait_ge(S("attention1_done"), 1)
            for e in range(E1 - LATE, E1, EB):
                sp.dma_start(w_dn1[:, e:e + EB], W_down[e:e + EB].rearrange("e f d -> f e d")).then_inc(S("w1_in"), 16)

            def experts1(n):
                for k in range(RING):
                    sp.wait_ge(S("y1"), n * RING + k + 1)
                    sp.dma_start(routed1[bass.ts(n * RING + k, P), :], y1[:, k]).then_inc(S(f"rows_out{k}"), 16)
            group_loop(sp, GROUPS1, experts1)

            def store_out(t):
                sp.wait_ge(S("final"), t + 1)
                sp.dma_start(out_t[bass.ts(t, 1)].rearrange("a p d -> (a p) d"), row(X, t)).then_inc(S("out_stored"), 16)
            with sp.Fori(0, NT, 1) as t:
                store_out(t)
            sp.wait_ge(S("out_stored"), 16 * NT)

        def route_counts(pe, E, NX, L):
            pe.wait_ge(S("sel_total"), L + 1)
            pe.matmul(bank(0)[0:E, 0:1], sel_sum[:, 0:E], ones16[:, 0:1], start=True, stop=True).then_inc(S("count_ps"), 1)
            pe.wait_ge(S("tiles"), 2 * (L + 1))
            pe.matmul(bank(1)[:, 0:E], tiles16[0:E, 1:1 + P], tri[0:E, 0:E], start=True, stop=True).then_inc(S("base_ps"), 1)
            pe.matmul(bank(2)[0:E, 0:1], triinc[0:E, 0:E], tiles16[0:E, 0:1], start=True, stop=True).then_inc(S("end_ps"), 1)
            pe.wait_ge(S("ended"), L + 1)
            pe.matmul(bank(3)[0:1, 0:NX], ones16[0:E, 0:1], ended[0:E, 0:NX], start=True, stop=True).then_inc(S("row_ps"), 1)

        def scalar_makes(k, L):
            return L == 1 and k % 2 == 1

        def route_table(pe, one_lo, one_hi, NX, pairs, L):
            def pair4(i, first, last):
                for k in range(4):
                    if scalar_makes(k, L):
                        pe.wait_ge(S("scalar_lo"), 2 * i + k // 2 + 1)
                    pe.wait_ge(S("one_hi"), NT * L + 4 * i + k + 1)
                    pe.matmul(bank(4)[:, 0:NX], one_lo[:, k, :], one_hi[:, k, 0:NX],
                              start=first and k == 0, stop=last and k == 3).then_inc(S("pair"), 1)
            n = pairs // 4
            pair4(0, True, False)
            with pe.Fori(1, n - 1, 1) as i:
                pair4(i, False, False)
            pair4(n - 1, False, True)

        def route_vector(dve, key, one_lo, one_hi, E, NX, per, L):
            n = NT * per
            dve.wait_ge(S("count_ps"), nth("count_ps", L + 1))
            dve.tensor_copy(tiles_of[0:E, 0:1], bank(0)[0:E, 0:1]).then_inc(S("count"), 1)
            dve.wait_ge(S("count"), nth("count", L + 1))
            dve.tensor_scalar(small[0:E, 0:NT], step128[0:E, :], tiles_of[0:E, 0:1], 0.0, ALU.is_lt, ALU.add,
                              accum_out=tiles_of[0:E, 1:2]).then_inc(S("ntiles"), 1)
            dve.wait_ge(S("ntiles"), nth("ntiles", L + 1))
            dve.tensor_copy(tiles16[0:E, 0:1], tiles_of[0:E, 1:2]).then_inc(S("tiles"), 1)
            dve.tensor_scalar(tiles16[0:E, 1:1 + P], ones16[0:E, :], tiles_of[0:E, 1:2], None, ALU.mult).then_inc(S("tiles"), 1)
            dve.wait_ge(S("base_ps"), nth("base_ps", L + 1))
            dve.tensor_scalar(base[:, 0:E], bank(1)[:, 0:E], float(P), 1.0, ALU.mult, ALU.add).then_inc(S("base"), 1)
            dve.wait_ge(S("end_ps"), nth("end_ps", L + 1))
            dve.tensor_copy(tiles_of[0:E, 2:3], bank(2)[0:E, 0:1]).then_inc(S("end"), 1)
            dve.wait_ge(S("end"), nth("end", L + 1))
            dve.tensor_scalar(ended[0:E, 0:NX], iota16[0:E, 0:NX], tiles_of[0:E, 2:3], None, ALU.is_ge).then_inc(S("ended"), 1)
            dve.wait_ge(S("base"), L + 1)
            dve.tensor_tensor(key, rank[:, :, 0:E], base[:, 0:E].unsqueeze(1).broadcast_to([P, NT, E]), ALU.add).then_inc(S("key_all"), 1)
            dve.wait_ge(S("key_all"), nth("key_all", L + 1))
            dve.tensor_tensor(key, key, sel[:, :, 0:E], ALU.mult).then_inc(S("key"), 1)
            dve.wait_ge(S("key"), nth("key", L + 1))
            if per == 1:
                dve.tensor_reduce(slots[:, 0:n], key, X_AXIS, ALU.max).then_inc(S("slots"), NT)
            else:
                for t in range(NT):
                    dve.max(slots[:, per * t:per * t + per], key[:, t, :]).then_inc(S("slots"), 1)
            dve.wait_ge(S("row_ps"), nth("row_ps", L + 1))
            dve.tensor_scalar(expert_of[:, 0:NX], bank(3)[0:1, 0:NX], float(E - 1), None, ALU.min).then_inc(S("expert_row"), 1)
            dve.wait_ge(S("slots"), NT * (L + 1))
            dve.tensor_scalar(slot_i[:, 0:n], slots[:, 0:n], -1.0, None, ALU.add).then_inc(S("slot_i"), 1)
            dve.wait_ge(S("slot_i"), nth("slot_i", L + 1))
            dve.tensor_scalar(tmp_i[:, 0:n], slot_i[:, 0:n], 7, None, ALU.arith_shift_right).then_inc(S("hi_i"), 1)
            dve.wait_ge(S("hi_i"), nth("hi_i", L + 1))
            dve.tensor_copy(slot_hi[:, 0:n], tmp_i[:, 0:n]).then_inc(S("hi"), 1)
            dve.wait_ge(S("hi"), nth("hi", L + 1))
            dve.tensor_scalar(slot_lo[:, 0:n], slot_hi[:, 0:n], -float(P), -1.0, ALU.mult, ALU.add).then_inc(S("lo_"), 1)
            dve.wait_ge(S("lo_"), nth("lo_", L + 1))
            dve.tensor_tensor(slot_lo[:, 0:n], slots[:, 0:n], slot_lo[:, 0:n], ALU.add).then_inc(S("lo"), 1)
            dve.wait_ge(S("lo"), nth("lo", L + 1))

            def pair4(i, t=None):
                for k in range(4):
                    m = 4 * i + k
                    if some(NT * L + m - 3):
                        dve.wait_ge(S("pair"), NT * L + m - 3)
                    if not scalar_makes(k, L):
                        dve.tensor_scalar(one_lo[:, k, :], iota16[:, 0:P], slot_lo[:, bass.ts(m, 1)], None, ALU.is_equal).then_inc(S("one_lo"), 1)
                    tok = token_id[:, bass.ts(m if t is None else t, 1)]
                    dve.tensor_scalar(one_hi[:, k, 0:NX], iota16[:, 0:NX], slot_hi[:, bass.ts(m, 1)], tok, ALU.is_equal, ALU.mult).then_inc(S("one_hi"), 1)
            if per == 1:
                pair4(0)
                with dve.Fori(1, n // 4, 1) as i:
                    pair4(i)
            else:
                def tile8(t):
                    pair4(2 * t, t)
                    pair4(2 * t + 1, t)
                tile8(0)
                with dve.Fori(1, NT, 1) as t:
                    tile8(t)
            if some(NT * L + n):
                dve.wait_ge(S("pair"), NT * L + n)
            dve.tensor_copy(token_of[:, 0:NX], bank(4)[:, 0:NX]).then_inc(S("table"), 1)

        @block.tensor
        def _(pe):
            pe.wait_ge(S("ctx_in"), 16 * (NB + 6))
            for b in range(NB):
                for m in range(KC):
                    for c in range(KC):
                        i = pe.matmul(bank(2 * b + m)[:, 0:S2], wk[:, c, m * P:(m + 1) * P], cT[:, b, c, :], start=(c == 0), stop=(c == KC - 1))
                    i.then_inc(S("kT_ps"), 1)
            for b in range(NB):
                pe.wait_ge(S("kT"), KC * (b + 1))
                for m in range(KC):
                    for c in range(KC):
                        i = pe.matmul(bank(4 + 2 * b + m)[:, 0:S2], wq[:, c, m * P:(m + 1) * P], kT[:, b, c, :], start=(c == 0), stop=(c == KC - 1))
                    i.then_inc(S("qk_ps"), 1)
            for b in range(NB):
                for c in range(KC):
                    i = pe.matmul(bank(b)[0:1, 0:S2], bqc[:, c:c + 1], kT[:, b, c, :], start=(c == 0), stop=(c == KC - 1))
                i.then_inc(S("bqk_ps"), 1)
            for b in range(NB):
                for c in range(KC):
                    i = pe.matmul(bank(2 + b)[:, 0:D], cT[:, b, c, 0:P], wv[:, c, :], start=(c == 0), stop=(c == KC - 1))
                i.then_inc(S("v_ps"), 1)
            pe.wait_ge(S("qk"), NB * KC)
            for b in range(NB):
                for c in range(KC):
                    i = pe.matmul(bank(4 + b)[0:SL, 0:D], cT[:, b, c, P:S2], wv[:, c, :], start=(c == 0), stop=(c == KC - 1))
                i.then_inc(S("v_ps"), 1)

            def xn1_T(u):
                pe.wait_ge(S("xn1"), u + 1)
                if some(u):
                    pe.wait_ge(S("xn1T"), nth("xn1T", u))
                for c in range(KC):
                    i = pe.transpose(bank(0)[:, c * P:(c + 1) * P], xn1[:, c * P:(c + 1) * P], ident[:, :])
                i.then_inc(S("xn1T_ps"), 1)

            def scores0(u, b):
                pe.wait_ge(S("xn1T"), nth("xn1T", u + 1))
                if some(u):
                    pe.wait_ge(S("s0"), nth("s0", u))
                for c in range(KC):
                    pe.matmul(bank(1)[:, 0:S2], xn1T[:, c, :], qk[:, b, c, :], start=(c == 0), stop=False)
                pe.matmul(bank(1)[:, 0:S2], ones_row[:, :], bqk[0:1, b, :], start=False, stop=True).then_inc(S("s0_ps"), 1)

            def probs0_T(u):
                pe.wait_ge(S("p0"), nth("p0", u + 1))
                if some(u):
                    pe.wait_ge(S("p0T"), nth("p0T", u))
                for c in range(2):
                    i = pe.transpose(bank(2)[:, c * P:(c + 1) * P], p0[:, c, :], ident[:, :])
                i.then_inc(S("p0T_ps"), 1)

            def attend0(u, b):
                pe.wait_ge(S("p0T"), nth("p0T", u + 1))
                if some(u):
                    pe.wait_ge(S("x1"), nth("x1", u))
                for c in range(2):
                    i = pe.matmul(bank(3)[:, 0:D], p0T[:, c, :], v0[:, b, c, :], start=(c == 0), stop=(c == 1))
                i.then_inc(S("attn0_ps"), 1)

            def xn2_T(u):
                pe.wait_ge(S("xn2"), nth("xn2", u + 1))
                if some(u):
                    pe.wait_ge(S("xn2T"), u)
                for c in range(KC):
                    i = pe.transpose(bank(4)[:, c * P:(c + 1) * P], xn2[:, c * P:(c + 1) * P], ident[:, :])
                i.then_inc(S("xn2T_ps"), 1)

            def logits0(t):
                pe.wait_ge(S("xn2T"), t + 1)
                for c in range(KC):
                    i = pe.matmul(bank(4)[:, D:D + E0], xn2T[:, c, :], wr[:, c, :], start=(c == 0), stop=(c == KC - 1))
                i.then_inc(S("lg0_ps"), 1)

            def hidden0(t, w, b, name):
                if some(t):
                    pe.wait_ge(S("h0"), nth("h0", t))
                for f in range(FC0):
                    for c in range(KC):
                        i = pe.matmul(bank(b)[:, f * P:(f + 1) * P], w[:, c, f * P:(f + 1) * P], xn2T[:, c, :], start=(c == 0), stop=(c == KC - 1))
                i.then_inc(S(name), 1)

            def ranks0(t):
                if some(t):
                    pe.wait_ge(S("x1s"), t)
                pe.wait_ge(S("sel0"), nth("sel0", t + 1))
                if some(t):
                    pe.wait_ge(S("sel_sum0"), nth("sel_sum0", t))
                pe.matmul(bank(7)[:, 0:E0], tri[:, :], row(sel, t)[:, 0:E0], start=True, stop=False)
                pe.matmul(bank(7)[:, 0:E0], ones16[:, :], sel_sum[:, 0:E0], start=False, stop=True).then_inc(S("rank0_ps"), 1)

            def down0(t, half):
                if half == 0:
                    pe.wait_ge(S("h0"), nth("h0", t + 1))
                    pe.wait_ge(S("rank0"), nth("rank0", t + 1))
                for f in range(half * FC0 // 2, (half + 1) * FC0 // 2):
                    i = pe.matmul(bank(7)[:, 0:D], h0[:, f, :], wd[:, f, :], start=(f == 0), stop=(f == FC0 - 1))
                if half == 1:
                    i.then_inc(S("ffn0_ps"), 1)

            pe.wait_ge(S("v0"), 2 * NB)
            pe.wait_ge(S("bqk"), NB)
            pe.wait_ge(S("ffn0_in"), 16 * 4)
            xn1_T(0)
            scores0(0, 0)
            probs0_T(0)
            attend0(0, 0)
            xn1_T(1)
            scores0(1, 0)
            xn2_T(0)

            def ffn_and_next(t, b, b_scores, coming=2):
                logits0(t)
                hidden0(t, wg, 5, "gate0_ps")
                if coming >= 1:
                    probs0_T(t + 1)
                ranks0(t)
                if coming >= 1:
                    attend0(t + 1, b)
                if coming >= 2:
                    xn1_T(t + 2)
                hidden0(t, wu, 6, "up0_ps")
                if coming >= 2:
                    scores0(t + 2, b_scores)
                down0(t, 0)
                if coming >= 1:
                    xn2_T(t + 1)
                down0(t, 1)
            ffn_and_next(0, 0, 0)
            with pe.Fori(1, TPB - 2, 1) as t:
                ffn_and_next(t, 0, 0)
            ffn_and_next(TPB - 2, 0, NB - 1)
            with pe.Fori(TPB - 1, NT - 2, 1) as t:
                ffn_and_next(t, NB - 1, NB - 1)
            ffn_and_next(NT - 2, NB - 1, 0, 1)
            ffn_and_next(NT - 1, 0, 0, 0)

            pe.wait_ge(S("x1s"), NT)
            route_counts(pe, E0, NX0, 0)

            pe.wait_ge(S("fm_row"), 1)
            pe.matmul(bank(5)[:, 0:1], fmr[0:1, :], ones_row[0:1, 0:1], start=True, stop=True).then_inc(S("fmc_ps"), 1)
            pe.wait_ge(S("cL"), NB * KC)
            pe.wait_ge(S("fmc"), 1)

            def context_features(b):
                if some(b):
                    pe.wait_ge(S("kbd"), NG * HG * b)
                for g in range(NG):
                    i = pe.matmul(bank(5 + g // 2)[:, (g % 2) * S2:(g % 2 + 1) * S2], fm2[:, g % 2, :], cT[:, b, g // 2, :], start=True, stop=True)
                i.then_inc(S("kf_ps"), 1)
                if some(b):
                    pe.wait_ge(S("vb"), b)
                for g in range(NG):
                    pe.matmul(bank(7)[:, g * P:(g + 1) * P], cT[:, b, g // 2, 0:P], fm2[:, g % 2, :], start=True, stop=False)
                    i = pe.matmul(bank(7)[:, g * P:(g + 1) * P], ones_row[:, :], fmr[0:1, :], start=False, stop=True)
                i.then_inc(S("vf_ps"), 1)
                if some(b):
                    pe.wait_ge(S("vl"), b)
                pe.wait_ge(S("base"), 1)
                for g in range(NG):
                    pe.matmul(bank(1)[0:SL * HG, g * P:(g + 1) * P], cL[:, b, g // 2, :], fm2[:, g % 2, :], start=True, stop=False)
                    i = pe.matmul(bank(1)[0:SL * HG, g * P:(g + 1) * P], ones_row[:, 0:SL * HG], fmr[0:1, :], start=False, stop=True)
                i.then_inc(S("vl_ps"), 1)
            context_features(0)
            route_table(pe, one_lo0, one_hi0, NX0, NT, 0)
            context_features(1)

            def x0_T(n, k):
                j = n * RING + k
                p = k % 2
                pe.wait_ge(S(f"rows_in{k}"), 16 * (n + 1))
                if some(j - 1):
                    pe.wait_ge(S("x0T"), j - 1)
                for c in range(KC):
                    i = pe.transpose(bank(4 + p)[:, c * P:(c + 1) * P], g0[:, k, c * P:(c + 1) * P], ident[:, :])
                i.then_inc(S("x0T_ps"), 1)

            def gate_up0(n, k):
                j = n * RING + k
                p = k % 2
                pe.wait_ge(S(f"w0_in{k % WB}"), 32 * (n * (RING // WB) + k // WB + 1))
                pe.wait_ge(S("x0T"), j + 1)
                if some(j - 1):
                    pe.wait_ge(S("e0T"), j - 1)
                for half in range(2):
                    for f in range(FC0):
                        for c in range(KC):
                            at = half * F0 + f * P
                            i = pe.matmul(bank(2 * half + p)[:, f * P:(f + 1) * P], expert_w[k % WB][0][:, c, at:at + P], x0T[:, p, c, :], start=(c == 0), stop=(c == KC - 1))
                    i.then_inc(S("eg0_ps" if half == 0 else "eu0_ps"), 1)

            def expert_down0(n, k):
                j = n * RING + k
                p = k % 2
                pe.wait_ge(S("e0T"), j + 1)
                if some(j - 1):
                    pe.wait_ge(S("y0"), j - 1)
                for f in range(FC0):
                    i = pe.matmul(bank(6 + p)[:, 0:D], e0T[:, p, f, :], expert_w[k % WB][1][:, f, :], start=(f == 0), stop=(f == FC0 - 1))
                i.then_inc(S("dn0"), 1)

            def experts0(n):
                for k in range(RING):
                    gate_up0(n, k)
                    if k + 1 < RING:
                        x0_T(n, k + 1)
                    elif not (isinstance(n, int) and n == GROUPS0 - 1):
                        x0_T(n + 1, 0)
                    if k > 0:
                        expert_down0(n, k - 1)
                    elif not (isinstance(n, int) and n == 0):
                        expert_down0(n - 1, RING - 1)
            pe.wait_ge(S("table"), 1)
            pe.wait_ge(S("expert_row"), 1)
            pe.wait_ge(S("kbd"), NB * NG * HG)
            pe.wait_ge(S("vb"), NB)
            pe.wait_ge(S("vl"), NB)
            x0_T(0, 0)
            group_loop(pe, GROUPS0, experts0)
            expert_down0(GROUPS0 - 1, RING - 1)

            pe.wait_ge(S("y0"), NX0)
            pe.wait_ge(S("small1_in"), 16 * 6)

            def xn3_T(u):
                pe.wait_ge(S("xn3"), nth("xn3", u + 1))
                for c in range(KC):
                    i = pe.transpose(bank(7)[:, c * P:(c + 1) * P], xn3[:, c * P:(c + 1) * P], ident[:, :])
                i.then_inc(S("xn3T_ps"), 1)

            def features(u):
                pe.wait_ge(S("xn3T"), u + 1)
                for g in range(NG):
                    i = pe.matmul(bank(7)[:, g * P:(g + 1) * P], fm2[:, g % 2, :], xn3T[:, g // 2, :], start=True, stop=True)
                i.then_inc(S("qf_ps"), 1)

            def scores1(t, g, b):
                s = 2 * (g % 2)
                pe.wait_ge(S("qf"), t + 1)
                if some(NG * t + g - 1):
                    pe.wait_ge(S("prob"), NG * t + g - 1)
                for h in range(HG):
                    i = pe.matmul(bank(s + h // 2)[:, (h % 2) * S2:(h % 2 + 1) * S2], qf[:, g, :], kbd[:, b, HG * g + h, :], start=True, stop=True)
                i.then_inc(S("s1_ps"), 1)

            def probs1_T(t, g):
                p = g % 2
                pe.wait_ge(S("prob"), NG * t + g + 1)
                if some(NG * t + g):
                    pe.wait_ge(S("probT"), NG * t + g)
                for h in range(HG):
                    i = pe.transpose(bank(4)[:, h * P:(h + 1) * P], prob[:, p].rearrange("p (k h) -> p h k", h=HG)[:, h, 0:P], ident[:, :])
                i.then_inc(S("probT_ps"), 1)
                if some(NG * t + g):
                    pe.wait_ge(S("leftT"), NG * t + g)
                pe.transpose(bank(5)[0:SL * HG, 0:P], prob[:, p, P * HG:S2 * HG], ident[:, :]).then_inc(S("leftT_ps"), 1)

            def attend1(t, g, b):
                p = g % 2
                pe.wait_ge(S("leftT"), NG * t + g + 1)
                pe.wait_ge(S("probT"), NG * t + g + 1)
                if g % 2 == 0:
                    if some((NG // 2) * t + g // 2):
                        pe.wait_ge(S("of"), (NG // 2) * t + g // 2)
                o = bank(6)[:, p * HG * VW:(p + 1) * HG * VW]
                pe.matmul(o, leftT[0:SL * HG, p, :], vl[0:SL * HG, b, HG * g:HG * (g + 1), :].rearrange("p h v -> p (h v)"), start=True, stop=True)
                for h in range(HG):
                    i = pe.matmul(o[:, h * VW:(h + 1) * VW], probT[:, p, h, :], vb[:, b, HG * g + h, :], start=False, stop=True, skip_group_check=True)
                i.then_inc(S("o_ps"), 1)

            def of_T(t):
                pe.wait_ge(S("of"), (NG // 2) * (t + 1))
                for g in range(NG):
                    i = pe.transpose(bank(7)[:, g * P:(g + 1) * P], of[:, HG * g:HG * (g + 1), :].rearrange("p h f -> p (h f)"), ident[:, :])
                i.then_inc(S("ofT_ps"), 1)

            def project(t):
                pe.wait_ge(S("ofT"), t + 1)
                for g in range(NG):
                    i = pe.matmul(bank(7)[:, 0:D], ofT[:, g, :], fcw[:, g, :], start=(g == 0), stop=(g == NG - 1))
                i.then_inc(S("fc_ps"), 1)

            def xn4_T(t):
                pe.wait_ge(S("xn4"), nth("xn4", t + 1))
                for c in range(KC):
                    i = pe.transpose(bank(7)[:, c * P:(c + 1) * P], xn4[:, c * P:(c + 1) * P], ident[:, :])
                i.then_inc(S("xn4T_ps"), 1)

            def logits1(t):
                pe.wait_ge(S("xn4T"), t + 1)
                for c in range(KC):
                    pe.matmul(bank(7)[:, 0:E1], xn4T[:, c, :], cen[:, c, :], start=(c == 0), stop=(c == KC - 1))
                for c in range(KC):
                    i = pe.matmul(bank(7)[:, E1:E1 + P], wsu[:, c, :], xn4T[:, c, :], start=(c == 0), stop=(c == KC - 1))
                i.then_inc(S("lg1_ps"), 1)

            def shared1(t):
                pe.wait_ge(S("sel1"), nth("sel1", t + 1))
                pe.wait_ge(S("aff"), t + 1)
                pe.matmul(bank(7)[:, 0:D], hs1T, wsd, start=True, stop=True).then_inc(S("ffn1_ps"), 1)

            def ranks1(t):
                if some(t):
                    pe.wait_ge(S("sel_sum1"), nth("sel_sum1", t))
                pe.matmul(bank(7)[:, D:D + E1], tri[:, :], row(sel, t), start=True, stop=False)
                pe.matmul(bank(7)[:, D:D + E1], ones16[:, :], sel_sum[:, :], start=False, stop=True).then_inc(S("rank1_ps"), 1)

            def back_end1(t):
                shared1(t)
                ranks1(t)

            def attention1(t, b, b_next, behind=2, coming=True):
                scores1(t, 2, b)
                scores1(t, 3, b)
                if behind >= 2:
                    back_end1(t - 2)
                attend1(t, 0, b)
                if behind >= 2:
                    pe.wait_ge(S("x3s"), t - 1)
                    pe.wait_ge(S("rank1"), nth("rank1", t - 1))
                if coming:
                    xn3_T(t + 1)
                probs1_T(t, 1)
                if coming:
                    features(t + 1)
                attend1(t, 1, b)
                if behind:
                    if coming:
                        pe.wait_ge(S("qf"), t + 2)
                    of_T(t - 1)
                probs1_T(t, 2)
                if coming:
                    scores1(t + 1, 0, b_next)
                if behind:
                    project(t - 1)
                attend1(t, 2, b)
                probs1_T(t, 3)
                if coming:
                    scores1(t + 1, 1, b_next)
                if behind:
                    xn4_T(t - 1)
                attend1(t, 3, b)
                if behind:
                    logits1(t - 1)
                if coming:
                    probs1_T(t + 1, 0)

            xn3_T(0)
            features(0)
            scores1(0, 0, 0)
            scores1(0, 1, 0)
            probs1_T(0, 0)
            attention1(0, 0, 0, behind=0)
            attention1(1, 0, 0, behind=1)
            attention1(2, 0, 0)
            with pe.Fori(3, TPB - 1, 1) as t:
                attention1(t, 0, 0)
            attention1(TPB - 1, 0, NB - 1)
            with pe.Fori(TPB, NT - 1, 1) as t:
                attention1(t, NB - 1, NB - 1)
            attention1(NT - 1, NB - 1, NB - 1, coming=False)
            t = NT - 1
            back_end1(t - 1)
            pe.wait_ge(S("x3s"), t)
            pe.wait_ge(S("rank1"), nth("rank1", t))
            of_T(t)
            project(t)
            xn4_T(t)
            logits1(t)
            back_end1(t)
            pe.wait_ge(S("rank1"), nth("rank1", NT))
            route_counts(pe, E1, NX1, 1)
            route_table(pe, one_lo1, one_hi1, NX1, NT * TOP1, 1)

            def x1_T(n, k):
                j = n * RING + k
                p = k % 2
                pe.wait_ge(S(f"rows_in{k}"), 16 * (n + 1 + GROUPS0))
                for c in range(KC):
                    i = pe.transpose(bank(p)[:, c * P:(c + 1) * P], g1[:, k, c * P:(c + 1) * P], ident[:, :])
                i.then_inc(S("x1T_ps"), 1)

            def experts(at, count):
                _, e = nc.values_load_multi_w_load_instructions(expert_of[0:1, bass.ds(at, count)], engines=(pe.engine,), min_val=0, max_val=E1 - 1,
                                                                    skip_runtime_bounds_check_because="the row counts experts and stops at the last")
                return e

            def up1(n, k, e):
                j = n * RING + k
                p = k % 2
                pe.wait_ge(S("x1T"), j + 1)
                for c in range(KC):
                    i = pe.matmul(bank(2 + p)[:, 0:F1], x1T[:, p, c, :], w_up1[:, bass.ts(e, 1), c, :], start=(c == 0), stop=(c == KC - 1))
                i.then_inc(S("up1_ps"), 1)

            def h1_T(n, k):
                j = n * RING + k
                p = k % 2
                pe.wait_ge(S("h1"), j + 1)
                pe.transpose(bank(4 + p)[:, 0:P], h1[:, p, :], ident[:, :]).then_inc(S("h1T_ps"), 1)

            def down1(n, k, e):
                j = n * RING + k
                p = k % 2
                pe.wait_ge(S("h1T"), j + 1)
                if some(j - 1):
                    pe.wait_ge(S("y1"), j - 1)
                pe.matmul(bank(6 + p)[:, 0:D], h1T[:, p, :], w_dn1[:, bass.ts(e, 1), :], start=True, stop=True).then_inc(S("dn1_ps"), 1)

            kept = [pe.alloc_register(f"kept{i}") for i in range(2)]

            def experts1(n):
                first, final = (isinstance(n, int) and n == at for at in (0, GROUPS1 - 1))
                e = [experts(n * RING, 1)[0]]
                for k in range(RING):
                    up1(n, k, e[k])
                    if k + 1 < RING:
                        e += experts(n * RING + k + 1, 1)
                    if k + 2 < RING:
                        x1_T(n, k + 2)
                    elif not final:
                        x1_T(n + 1, k + 2 - RING)
                    if k >= 1:
                        h1_T(n, k - 1)
                    elif not first:
                        h1_T(n - 1, RING - 1)
                    if k >= 2:
                        down1(n, k - 2, e[k - 2])
                    elif not first:
                        down1(n - 1, k + RING - 2, pe.snap(kept[k], min_val=0, max_val=E1 - 1))
                if not final:
                    for reg, at in zip(kept, e[RING - 2:]):
                        pe.reg_mov(reg, at)
            pe.wait_ge(S("w1_in"), 16 * (E1 // 8) * (KC + 1))
            pe.wait_ge(S("table"), 2)
            pe.wait_ge(S("expert_row"), 2)
            x1_T(0, 0)
            x1_T(0, 1)
            group_loop(pe, GROUPS1, experts1)
            n = GROUPS1 - 1
            h1_T(n, RING - 1)
            before = experts(n * RING + RING - 2, 2)
            down1(n, RING - 2, before[0])
            down1(n, RING - 1, before[1])

        @block.scalar
        def _(act):
            for i in range(4):
                n = NT // 4
                act.dma_start(X[:, n * i:n * i + n, :], x_t[:, n * i:n * i + n, :]).then_inc(S("x_in"), 16)
            for b in range(NB):
                for m in range(KC):
                    act.wait_ge(S("qk_ps"), KC * b + m + 1)
                    act.activation(qk[:, b, m, :], bank(4 + 2 * b + m)[:, 0:S2], ACT.Copy, scale=QS).then_inc(S("qk"), 1)
            for b in range(NB):
                act.wait_ge(S("bqk_ps"), b + 1)
                act.activation(bqk[0:1, b, :], bank(b)[0:1, 0:S2], ACT.Copy, scale=QS).then_inc(S("bqk"), 1)

            def xn1_T(u):
                act.wait_ge(S("xn1T_ps"), nth("xn1T_ps", u + 1))
                if some(u):
                    act.wait_ge(S("s0_ps"), nth("s0_ps", u))
                act.activation(xn1T.rearrange("p c n -> p (c n)"), bank(0)[:, 0:D], ACT.Copy).then_inc(S("xn1T"), 1)

            def probs0(u):
                act.wait_ge(S("nm0"), nth("nm0", u + 1))
                if some(u):
                    act.wait_ge(S("p0T_ps"), nth("p0T_ps", u))
                if some(u):
                    act.wait_ge(S("rinv0"), nth("rinv0", u))
                act.activation(p0.rearrange("p c n -> p (c n)")[:, 0:S2], s0, ACT.Exp, bias=nm0[:, :], accum_out=rsum[:, :]).then_inc(S("p0"), 1)

            def probs0_T(u):
                act.wait_ge(S("p0T_ps"), nth("p0T_ps", u + 1))
                if some(u):
                    act.wait_ge(S("attn0_ps"), nth("attn0_ps", u))
                act.activation(p0T.rearrange("p c n -> p (c n)"), bank(2)[:, 0:2 * P], ACT.Copy).then_inc(S("p0T"), 1)

            def xn2_T(u):
                act.wait_ge(S("xn2T_ps"), nth("xn2T_ps", u + 1))
                if some(u):
                    act.wait_ge(S("up0_ps"), nth("up0_ps", u))
                act.activation(xn2T.rearrange("p c n -> p (c n)"), bank(4)[:, 0:D], ACT.Copy).then_inc(S("xn2T"), 1)

            def score0(t):
                act.wait_ge(S("best0"), nth("best0", t + 1))
                if some(t):
                    act.wait_ge(S("score0"), nth("score0", t))
                act.activation(sg_e[:, 0:1], best[:, 0:1], ACT.Exp, scale=-1.0).then_inc(S("sg0"), 1)

            def gate0(t):
                act.wait_ge(S("gate0_ps"), nth("gate0_ps", t + 1))
                if some(t):
                    act.wait_ge(S("ha0"), nth("ha0", t))
                act.activation(th0, bank(5), ACT.Tanh, scale=0.5).then_inc(S("th0"), 1)

            xn1_T(0)
            probs0(0)
            probs0_T(0)
            xn1_T(1)
            probs0(1)
            xn2_T(0)

            def ffn_and_next(t, coming=2):
                score0(t)
                if coming >= 1:
                    probs0_T(t + 1)
                gate0(t)
                if coming >= 2:
                    xn1_T(t + 2)
                    probs0(t + 2)
                if coming >= 1:
                    xn2_T(t + 1)
            ffn_and_next(0)
            with act.Fori(1, NT - 2, 1) as t:
                ffn_and_next(t)
            ffn_and_next(NT - 2, 1)
            ffn_and_next(NT - 1, 0)

            act.wait_ge(S("fmc_ps"), 1)
            act.activation(fmc, bank(5)[:, 0:1], ACT.Copy).then_inc(S("fmc"), 1)
            act.wait_ge(S("fmc"), 1)
            act.wait_ge(S("log_scale"), 2)
            act.activation(fmk, fmc, ACT.Identity, bias=log_scale[:, :]).then_inc(S("fmk"), 1)
            act.wait_ge(S("fmk"), 1)
            act.wait_ge(S("setup1_zeroed"), 3)
            for b in range(NB):
                act.wait_ge(S("kf_ps"), b + 1)
                for g in range(NG):
                    for h in range(HG):
                        rows = slice(FD * h, FD * h + FD)
                        act.activation(kbd[rows, b, HG * g + h, :], bank(5 + g // 2)[rows, (g % 2) * S2:(g % 2 + 1) * S2], ACT.Exp,
                                       bias=fmk[rows, :]).then_inc(S("kbd"), 1)
                act.wait_ge(S("vf_ps"), b + 1)
                act.activation(vb[:, b, :, 0:FD], bank(7).rearrange("p (h f) -> p h f", h=NH), ACT.Exp).then_inc(S("vb"), 1)
                act.wait_ge(S("vl_ps"), b + 1)
                act.activation(vl[0:SL * HG, b, :, 0:FD], bank(1)[0:SL * HG, :].rearrange("p (h f) -> p h f", h=NH), ACT.Exp).then_inc(S("vl"), 1)

            def x0_T(n, k):
                j = n * RING + k
                act.wait_ge(S("x0T_ps"), j + 1)
                if some(j - 1):
                    act.wait_ge(S("eu0_ps"), j - 1)
                act.activation(x0T[:, k % 2].rearrange("p c n -> p (c n)"), bank(4 + k % 2)[:, 0:D], ACT.Copy).then_inc(S("x0T"), 1)

            def silu0(n, k):
                j = n * RING + k
                act.wait_ge(S("eg0_ps"), j + 1)
                if some(j - 1):
                    act.wait_ge(S("e0T"), j - 1)
                act.activation(sg0[:, k % 2], bank(k % 2), ACT.Silu).then_inc(S("sg0x"), 1)

            def experts0(n):
                for k in range(RING):
                    silu0(n, k)
                    if k + 1 < RING:
                        x0_T(n, k + 1)
                    elif not (isinstance(n, int) and n == GROUPS0 - 1):
                        x0_T(n + 1, 0)
            x0_T(0, 0)
            group_loop(act, GROUPS0, experts0)

            def xn3_T(u):
                act.wait_ge(S("xn3T_ps"), nth("xn3T_ps", u + 1))
                act.activation(xn3T.rearrange("p c n -> p (c n)"), bank(7)[:, 0:D], ACT.Copy).then_inc(S("xn3T"), 1)

            def features(u):
                act.wait_ge(S("qf_ps"), nth("qf_ps", u + 1))
                if some(u):
                    act.wait_ge(S("s1_ps"), NG * u)
                act.activation(qf.rearrange("p g n -> p (g n)"), bank(7), ACT.Exp, bias=fmc).then_inc(S("qf"), 1)

            def probs1(t, g):
                act.wait_ge(S("nmax"), NG * t + g + 1)
                if some(NG * t + g - 1):
                    act.wait_ge(S("leftT_ps"), NG * t + g - 1)
                for h in range(HG):
                    src = bank(2 * (g % 2) + h // 2)[:, (h % 2) * S2:(h % 2 + 1) * S2]
                    i = act.activation(prob[:, g % 2].rearrange("p (k h) -> p h k", h=HG)[:, h, :], src, ACT.Exp, bias=nmax2[:, g % 2, h:h + 1])
                i.then_inc(S("prob"), 1)

            def probs1_T(t, g):
                act.wait_ge(S("leftT_ps"), NG * t + g + 1)
                if some(NG * t + g - 1):
                    act.wait_ge(S("o_ps"), NG * t + g - 1)
                act.activation(leftT[0:SL * HG, g % 2], bank(5)[0:SL * HG, 0:P], ACT.Copy).then_inc(S("leftT"), 1)

            def xn4_T(t):
                act.wait_ge(S("xn4T_ps"), nth("xn4T_ps", t + 1))
                act.activation(xn4T.rearrange("p c n -> p (c n)"), bank(7)[:, 0:D], ACT.Copy).then_inc(S("xn4T"), 1)

            def of_T(t):
                act.wait_ge(S("ofT_ps"), nth("ofT_ps", t + 1))
                if some(t):
                    act.wait_ge(S("fc_ps"), nth("fc_ps", t))
                act.activation(ofT.rearrange("p g n -> p (g n)"), bank(7), ACT.Copy).then_inc(S("ofT"), 1)

            def logits1(t):
                act.wait_ge(S("lg1_ps"), nth("lg1_ps", t + 1))
                if some(t):
                    act.wait_ge(S("hs1"), nth("hs1", t))
                act.activation(th1, bank(7)[:, E1:E1 + P], ACT.Tanh, scale=0.5).then_inc(S("th1"), 1)
                act.activation(row(weight, t), bank(7)[:, 0:E1], ACT.Copy).then_inc(S("aff"), 1)

            def attention1(t, behind=True, coming=True):
                probs1(t, 2)
                if coming:
                    xn3_T(t + 1)
                probs1_T(t, 1)
                if coming:
                    features(t + 1)
                probs1(t, 3)
                if behind:
                    of_T(t - 1)
                probs1_T(t, 2)
                if coming:
                    probs1(t + 1, 0)
                probs1_T(t, 3)
                if behind:
                    xn4_T(t - 1)
                if coming:
                    probs1(t + 1, 1)
                if behind:
                    logits1(t - 1)
                if coming:
                    probs1_T(t + 1, 0)
            xn3_T(0)
            features(0)
            probs1(0, 0)
            probs1(0, 1)
            probs1_T(0, 0)
            attention1(0, behind=False)
            attention1(1)
            with act.Fori(2, NT - 1, 1) as t:
                attention1(t)
            attention1(NT - 1, coming=False)
            of_T(NT - 1)
            xn4_T(NT - 1)
            logits1(NT - 1)
            act.wait_ge(S("aff"), NT)
            act.activation(weight[:, :, :], weight[:, :, :], ACT.Exp, scale=-1.0).then_inc(S("w_exp"), 1)

            def one_lo2(i):
                for k in (1, 3):
                    m = 4 * i + k
                    act.wait_ge(S("pair"), NT + m - 3)
                    act.activation(away[:, k // 2, :], iota16[:, 0:P], ACT.Abs, scale=-1.0, bias=slot_lo[:, bass.ts(m, 1)]).then_inc(S("away"), 1)
                for k in (1, 3):
                    act.wait_ge(S("away"), 2 * i + k // 2 + 1)
                    act.activation(one_lo1[:, k, :], away[:, k // 2, :], ACT.Relu, scale=-1.0, bias=one_col[:, :]).then_inc(S("scalar_lo"), 1)
            act.wait_ge(S("lo"), nth("lo", 2))
            one_lo2(0)
            with act.Fori(1, NT * TOP1 // 4, 1) as i:
                one_lo2(i)

            def x1_T(n, k):
                j = n * RING + k
                act.wait_ge(S("x1T_ps"), j + 1)
                act.activation(x1T[:, k % 2].rearrange("p c n -> p (c n)"), bank(k % 2)[:, 0:D], ACT.Copy).then_inc(S("x1T"), 1)

            def silu1(n, k):
                j = n * RING + k
                act.wait_ge(S("up1_ps"), j + 1)
                if some(j - 1):
                    act.wait_ge(S("h1T_ps"), j - 1)
                act.activation(h1[:, k % 2, :], bank(2 + k % 2)[:, 0:F1], ACT.Silu).then_inc(S("h1"), 1)

            def experts1(n):
                for k in range(RING):
                    silu1(n, k)
                    if k + 2 < RING:
                        x1_T(n, k + 2)
                    elif not (isinstance(n, int) and n == GROUPS1 - 1):
                        x1_T(n + 1, k + 2 - RING)
            x1_T(0, 0)
            x1_T(0, 1)
            group_loop(act, GROUPS1, experts1)

        @block.vector
        def _(dve):
            dve.memset(ones16[:, :], 1.0).then_inc(S("dve_const"), 1)
            dve.memset(ones_row[:, :], 1.0).then_inc(S("dve_const"), 1)
            dve.memset(neg_half[:, :], -0.5).then_inc(S("neg_half"), 1)
            dve.memset(fm2, 0.0).then_inc(S("zeroed"), 1)
            dve.memset(p0, 0.0).then_inc(S("dve_const"), 1)
            dve.memset(v0[:, :, 1, :], 0.0).then_inc(S("dve_const"), 1)
            dve.memset(sel_sum[:, :], 0.0).then_inc(S("dve_const"), 1)

            dve.wait_ge(S("x_in"), 64)

            for t in range(NT):
                dve.bn_stats(weight[:, t, 0:6], X[:, t, :]).then_inc(S("stats1"), 1)
            for t in range(NT):
                dve.wait_ge(S("stats1"), t + 1)
                dve.bn_aggr(mv_all[:, t, :], weight[:, t, 0:6]).then_inc(S("mv1"), 1)
            dve.wait_ge(S("mv1"), NT)
            dve.tensor_scalar(rstd_all[:, :], mv_all[:, :, 1], LN_EPS, None, ALU.add).then_inc(S("var1"), 1)
            dve.wait_ge(S("dve_const"), 5)
            dve.wait_ge(S("ctx_in"), 16 * (NB + 6))
            for b in range(NB):
                for m in range(KC):
                    dve.wait_ge(S("kT_ps"), KC * b + m + 1)
                    dve.tensor_scalar(kT[:, b, m, :], bank(2 * b + m)[:, 0:S2], bkc[:, m:m + 1], None, ALU.add).then_inc(S("kT"), 1)
            for b in range(NB):
                dve.wait_ge(S("v_ps"), b + 1)
                dve.tensor_tensor(v0[:, b, 0, :], bank(2 + b)[:, 0:D], bvb, ALU.add).then_inc(S("v0"), 1)
            for b in range(NB):
                dve.wait_ge(S("v_ps"), NB + b + 1)
                dve.tensor_tensor(v0[0:SL, b, 1, :], bank(4 + b)[0:SL, 0:D], bvb[0:SL, :], ALU.add).then_inc(S("v0"), 1)
            dve.wait_ge(S("rstd1"), 1)
            dve.wait_ge(S("mask_in"), 16)

            def norm1(u):
                if some(u):
                    dve.wait_ge(S("xn1T_ps"), nth("xn1T_ps", u))
                dve.tensor_scalar(xn1, row(X, u), row(mv_all, u)[:, 0:1], rstd_all[:, bass.ts(u, 1)], ALU.subtract, ALU.mult).then_inc(S("xn1"), 1)

            def softmax0(u, m):
                dve.wait_ge(S("s0_ps"), nth("s0_ps", u + 1))
                if some(u):
                    dve.wait_ge(S("p0"), nth("p0", u))
                dve.scalar_tensor_tensor(s0, row(msk, m), MASKED, bank(1)[:, 0:S2], ALU.mult, ALU.add).then_inc(S("s0"), 1)
                dve.wait_ge(S("s0"), nth("s0", u + 1))
                dve.tensor_reduce(nm0[:, :], s0, X_AXIS, ALU.max, negate=True).then_inc(S("nm0"), 1)

            def residual1(u):
                dve.wait_ge(S("p0"), nth("p0", u + 1))
                dve.reciprocal(rinv[:, :], rsum[:, :]).then_inc(S("rinv0"), 1)
                dve.wait_ge(S("attn0_ps"), nth("attn0_ps", u + 1))
                dve.wait_ge(S("rinv0"), nth("rinv0", u + 1))
                dve.scalar_tensor_tensor(row(X, u), bank(3)[:, 0:D], rinv[:, :], row(X, u), ALU.mult, ALU.add).then_inc(S("x1"), 1)
                dve.wait_ge(S("x1"), nth("x1", u + 1))
                dve.sem_inc(S("waited_dve"), 1)
                norm_stats(u, "2")

            def norm_stats(t, name):
                dve.bn_stats(stats[:, :], row(X, t)).then_inc(S("stats" + name), 1)
                dve.wait_ge(S("stats" + name), nth("stats" + name, t + 1))
                dve.sem_inc(S("waited_dve"), 1)
                dve.bn_aggr(mv[:, :], stats[:, :]).then_inc(S("mv" + name), 1)
                dve.wait_ge(S("mv" + name), nth("mv" + name, t + 1))
                dve.tensor_scalar(var_eps[:, :], mv[:, 1:2], LN_EPS, None, ALU.add).then_inc(S("var" + name), 1)

            def norm_apply(t, name, dst):
                dve.wait_ge(S("rstd" + name), t + 1)
                dve.tensor_scalar(dst, row(X, t), mv[:, 0:1], rstd[:, :], ALU.subtract, ALU.mult).then_inc(S("xn" + name), 1)

            def norm2(u):
                if some(u):
                    dve.wait_ge(S("xn2T_ps"), u)
                norm_apply(u, "2", xn2)

            def router0(t):
                dve.wait_ge(S("lg0_ps"), nth("lg0_ps", t + 1))
                if some(t):
                    dve.wait_ge(S("sel0"), nth("sel0", t))
                dve.tensor_copy(lg[:, 0:E0], bank(4)[:, D:D + E0]).then_inc(S("lg0"), 1)
                dve.wait_ge(S("lg0"), nth("lg0", t + 1))
                if some(t):
                    dve.wait_ge(S("sg0"), nth("sg0", t))
                dve.sem_inc(S("waited_dve"), 1)
                dve.max(best[:, :], lg[:, 0:E0]).then_inc(S("best0"), 1)
                dve.wait_ge(S("best0"), nth("best0", t + 1))
                dve.sem_inc(S("waited_dve"), 1)
                dve.max_index(best_i[:, :], best[:, :], lg[:, 0:E0]).then_inc(S("best_i0"), 1)
                dve.wait_ge(S("best_i0"), nth("best_i0", t + 1))
                dve.tensor_copy(small[:, 0:1], best_i[:, 0:1]).then_inc(S("top0"), 1)
                dve.wait_ge(S("top0"), nth("top0", t + 1))
                dve.tensor_scalar(row(sel, t)[:, 0:E0], iota16[:, 0:E0], small[:, 0:1], None, ALU.is_equal).then_inc(S("sel0"), 1)
                dve.wait_ge(S("sg0"), nth("sg0", t + 1))
                dve.tensor_scalar(sg_d[:, 0:1], sg_e[:, 0:1], 1.0, None, ALU.add).then_inc(S("sgd0"), 1)
                dve.wait_ge(S("sgd0"), nth("sgd0", t + 1))
                dve.reciprocal(sg_d[:, 1:2], sg_d[:, 0:1]).then_inc(S("score0"), 1)
                dve.wait_ge(S("score0"), nth("score0", t + 1))
                if some(t * 16):
                    dve.wait_ge(S("xs0_stored"), t * 16)
                dve.tensor_scalar(xs0, xn2, sg_d[:, 1:2], None, ALU.mult).then_inc(S("xs0"), 1)

            def ranks0(t):
                dve.wait_ge(S("rank0_ps"), nth("rank0_ps", t + 1))
                dve.tensor_copy(row(rank, t)[:, 0:E0], bank(7)[:, 0:E0]).then_inc(S("rank0"), 1)
                dve.tensor_tensor(sel_sum[:, 0:E0], sel_sum[:, 0:E0], row(sel, t)[:, 0:E0], ALU.add).then_inc(S("sel_sum0"), 1)

            def gated0(t):
                dve.wait_ge(S("th0"), nth("th0", t + 1))
                dve.scalar_tensor_tensor(a0, th0, 1.0, bank(5), ALU.add, ALU.mult).then_inc(S("ha0"), 1)

            def hidden0(t):
                dve.wait_ge(S("ha0"), nth("ha0", t + 1))
                dve.wait_ge(S("up0_ps"), nth("up0_ps", t + 1))
                if some(t):
                    dve.wait_ge(S("ffn0_ps"), nth("ffn0_ps", t))
                dve.scalar_tensor_tensor(h0.rearrange("p c n -> p (c n)"), a0, 0.5, bank(6), ALU.mult, ALU.mult).then_inc(S("h0"), 1)

            def shared0(t):
                dve.wait_ge(S("ffn0_ps"), nth("ffn0_ps", t + 1))
                dve.tensor_tensor(row(X, t), row(X, t), bank(7)[:, 0:D], ALU.add).then_inc(S("x1s"), 1)

            norm1(0)
            softmax0(0, 0)
            norm1(1)
            residual1(0)
            softmax0(1, 1)
            norm2(0)
            dve.wait_ge(S("consts"), 1)
            dve.tensor_reduce(head_of[:, :], head_at, X_AXIS, ALU.add).then_inc(S("head_of"), 1)

            def ffn_and_next(t, m, coming=2):
                if coming >= 2:
                    norm1(t + 2)
                router0(t)
                ranks0(t)
                gated0(t)
                if coming >= 1:
                    residual1(t + 1)
                hidden0(t)
                if coming >= 1:
                    norm2(t + 1)
                if coming >= 2:
                    softmax0(t + 2, m)
                shared0(t)
            ffn_and_next(0, 2)
            with dve.Fori(1, TPB - 2, 1) as t:
                ffn_and_next(t, t + 2)
            with dve.Fori(TPB - 2, NT - 2, 1) as t:
                ffn_and_next(t, t + 2 - TPB)
            ffn_and_next(NT - 2, 0, 1)
            ffn_and_next(NT - 1, 0, 0)
            dve.wait_ge(S("sel_sum0"), nth("sel_sum0", NT))
            dve.sem_inc(S("sel_total"), 1)

            dve.wait_ge(S("fm_in"), 16 * 2 * (P // HD))
            fmv = fm2.rearrange("p a (h s e) -> p a h s e", s=2, e=HD)
            for a in range(2):
                i = dve.tensor_scalar(fmv[:, a, :, 1, :], fmv[:, a, :, 0, :], -1.0, None, ALU.mult)
            fmrv = fmr[0:1, :].rearrange("p (h s e) -> p h s e", s=2, e=HD)
            dve.tensor_scalar(fmrv[:, :, 1, :], fmrv[:, :, 1, :], -1.0, None, ALU.mult).then_inc(S("fm_row"), 1)
            for b in range(NB):
                for c in range(KC):
                    dst = cL[:, b, c, :].rearrange("p (k h) -> p k h", h=HG)
                    dve.tensor_copy(dst, cT[:, b, c, P:S2].unsqueeze(2).broadcast_to([P, SL, HG])).then_inc(S("cL"), 1)

            route_vector(dve, key0, one_lo0, one_hi0, E0, NX0, 1, 0)
            dve.wait_ge(S("kbd"), NB * NG * HG)
            dve.wait_ge(S("vb"), NB)
            for b in range(NB):
                dve.wait_ge(S("vl"), b + 1)
                for h in range(HG):
                    dve.wait_ge(S("head_of"), 1)
                    own = vl[0:SL * HG, b, :, :].rearrange("p (g h) v -> p g h v", h=HG)[:, :, h, :]
                    dve.tensor_scalar(own, own, head_of[0:SL * HG, h:h + 1], None, ALU.mult).then_inc(S("vl_own"), 1)
            dve.wait_ge(S("vl_own"), NB * HG)
            dve.sem_inc(S("setup1_done"), 1)

            def hidden_x0(n, k):
                j = n * RING + k
                p = k % 2
                dve.wait_ge(S("sg0x"), j + 1)
                dve.wait_ge(S("eu0_ps"), j + 1)
                if some(j - 1):
                    dve.wait_ge(S("dn0"), j - 1)
                dve.tensor_tensor(e0T[:, p].rearrange("p c n -> p (c n)"), sg0[:, p], bank(2 + p), ALU.mult).then_inc(S("e0T"), 1)

            def out_x0(n, k):
                j = n * RING + k
                dve.wait_ge(S("dn0"), j + 1)
                if some(16 * n):
                    dve.wait_ge(S(f"rows_out{k}"), 16 * n)
                dve.tensor_copy(y0[:, k], bank(6 + k % 2)[:, 0:D]).then_inc(S("y0"), 1)

            def experts0(n):
                for k in range(RING):
                    hidden_x0(n, k)
                    if k > 0:
                        out_x0(n, k - 1)
                    elif not (isinstance(n, int) and n == 0):
                        out_x0(n - 1, RING - 1)
            group_loop(dve, GROUPS0, experts0)
            out_x0(GROUPS0 - 1, RING - 1)

            def residual2(u):
                dve.wait_ge(S("yg"), 16 * (u + 1))
                dve.tensor_tensor(row(X, u), row(X, u), yg, ALU.add).then_inc(S("x2"), 1)
                dve.wait_ge(S("x2"), nth("x2", u + 1))
                dve.sem_inc(S("waited_dve"), 1)
                norm_stats(u, "3")

            def norm3(u):
                if some(u):
                    dve.wait_ge(S("xn3T_ps"), nth("xn3T_ps", u))
                norm_apply(u, "3", xn3)
                dve.wait_ge(S("xn3"), nth("xn3", u + 1))
                dve.tensor_tensor(row(X, u), row(X, u), fcb, ALU.add).then_inc(S("x2b"), 1)

            def softmax1(t, g):
                dve.wait_ge(S("s1_ps"), NG * t + g + 1)
                if some(NG * t + g - 1):
                    dve.wait_ge(S("prob"), NG * t + g - 1)
                src = PS[:, 2 * (g % 2):2 * (g % 2) + 2, 0:2 * S2].rearrange("p b (h k) -> p b h k", h=2)
                dve.tensor_reduce(nmax2[:, g % 2, :].rearrange("p (b h) -> p b h", b=2), src, X_AXIS, ALU.max, negate=True).then_inc(S("nmax"), 1)

            def probs1_T(t, g):
                dve.wait_ge(S("probT_ps"), NG * t + g + 1)
                if some(NG * t + g - 1):
                    dve.wait_ge(S("o_ps"), NG * t + g - 1)
                dve.tensor_copy(probT[:, g % 2].rearrange("p h n -> p (h n)"), bank(4)).then_inc(S("probT"), 1)

            def heads(t, g):
                half = g // 2
                dve.wait_ge(S("o_ps"), NG * t + g + 1)
                if some((NG // 2) * t + half):
                    dve.wait_ge(S("of"), (NG // 2) * t + half)
                o = bank(6)[:, 0:2 * HG * VW].rearrange("p (h v) -> p h v", v=VW)
                dve.reciprocal(den[:, :], o[:, :, FD]).then_inc(S("den"), 1)
                dve.wait_ge(S("den"), (NG // 2) * t + half + 1)
                if half == 0:
                    if some(t):
                        dve.wait_ge(S("ofT_ps"), nth("ofT_ps", t))
                dve.tensor_tensor(of[:, 2 * HG * half:2 * HG * (half + 1), :], o[:, :, 0:FD], den[:, :].unsqueeze(2).broadcast_to([P, 2 * HG, FD]), ALU.mult).then_inc(S("of"), 1)

            def residual3(t):
                dve.wait_ge(S("fc_ps"), nth("fc_ps", t + 1))
                dve.wait_ge(S("x2b"), nth("x2b", t + 1))
                dve.tensor_tensor(row(X, t), row(X, t), bank(7)[:, 0:D], ALU.add).then_inc(S("x3"), 1)
                dve.wait_ge(S("x3"), nth("x3", t + 1))
                dve.sem_inc(S("waited_dve"), 1)
                norm_stats(t, "4")

            def norm4(t):
                if some(t):
                    dve.wait_ge(S("xn4T_ps"), nth("xn4T_ps", t))
                    dve.wait_ge(S("xn4_stored"), t * 16)
                norm_apply(t, "4", xn4)

            def router1(t):
                dve.wait_ge(S("lg1_ps"), nth("lg1_ps", t + 1))
                dve.wait_ge(S("th1"), t + 1)
                dve.wait_ge(S("aff"), t + 1)
                if some(t):
                    dve.wait_ge(S("ffn1_ps"), nth("ffn1_ps", t))
                dve.scalar_tensor_tensor(hs1T, th1, 1.0, bank(7)[:, E1:E1 + P], ALU.add, ALU.mult).then_inc(S("hs1"), 1)
                if some(t):
                    dve.wait_ge(S("sel1"), nth("sel1", t))
                dve.tensor_tensor(lg2[:, :], bank(7)[:, 0:E1], ebb, ALU.add).then_inc(S("biased"), 1)
                dve.wait_ge(S("biased"), nth("biased", t + 1))
                dve.sem_inc(S("waited_dve"), 1)
                dve.max(best[:, :], lg2[:, :]).then_inc(S("best1"), 1)
                dve.wait_ge(S("best1"), nth("best1", t + 1))
                dve.sem_inc(S("waited_dve"), 1)
                dve.match_replace(small[:, :], best[:, :], lg2[:, :], -3.0e38).then_inc(S("rep1"), 1)
                dve.wait_ge(S("rep1"), nth("rep1", t + 1))
                dve.tensor_tensor(row(sel, t), small[:, :], lg2[:, :], ALU.not_equal).then_inc(S("sel1"), 1)

            def back_end1(t):
                dve.wait_ge(S("rank1_ps"), nth("rank1_ps", t + 1))
                dve.scalar_tensor_tensor(row(X, t), bank(7)[:, 0:D], 0.5, row(X, t), ALU.mult, ALU.add).then_inc(S("x3s"), 1)
                dve.tensor_copy(row(rank, t), bank(7)[:, D:D + E1]).then_inc(S("rank1"), 1)
                dve.tensor_tensor(sel_sum[:, :], sel_sum[:, :], row(sel, t), ALU.add).then_inc(S("sel_sum1"), 1)

            def attention1(t, behind=2, coming=2):
                softmax1(t, 2)
                softmax1(t, 3)
                if behind >= 2:
                    back_end1(t - 2)
                if coming >= 2:
                    residual2(t + 2)
                probs1_T(t, 1)
                if coming >= 2:
                    norm3(t + 2)
                heads(t, 1)
                probs1_T(t, 2)
                if coming >= 1:
                    softmax1(t + 1, 0)
                if behind:
                    residual3(t - 1)
                probs1_T(t, 3)
                if behind:
                    norm4(t - 1)
                if coming >= 1:
                    softmax1(t + 1, 1)
                heads(t, 3)
                if coming >= 1:
                    probs1_T(t + 1, 0)
                if behind:
                    router1(t - 1)

            dve.wait_ge(S("small1_in"), 16 * 6)
            dve.memset(sel_sum[:, :], 0.0).then_inc(S("sums_zeroed"), 1)
            dve.wait_ge(S("sums_zeroed"), 1)
            residual2(0)
            norm3(0)
            residual2(1)
            norm3(1)
            softmax1(0, 0)
            softmax1(0, 1)
            probs1_T(0, 0)
            attention1(0, behind=0)
            attention1(1, behind=1)
            attention1(2)
            with dve.Fori(3, NT - 2, 1) as t:
                attention1(t)
            attention1(NT - 2, coming=1)
            attention1(NT - 1, coming=0)
            t = NT - 1
            back_end1(t - 1)
            residual3(t)
            norm4(t)
            router1(t)
            back_end1(t)
            dve.wait_ge(S("sel_sum1"), nth("sel_sum1", NT))
            dve.wait_ge(S("x3s"), NT)
            dve.sem_inc(S("attention1_done"), 1)
            dve.wait_ge(S("xn4_stored"), 16 * NT)
            dve.sem_inc(S("sel_total"), 1)

            route_vector(dve, slot_key, one_lo1, one_hi1, E1, NX1, TOP1, 1)

            dve.wait_ge(S("w_exp"), 1)
            dve.tensor_scalar(weight[:, :, :], weight[:, :, :], 1.0, None, ALU.add).then_inc(S("w_exp1"), 1)
            dve.wait_ge(S("w_exp1"), nth("w_exp1", 1))
            dve.reciprocal(weight[:, :, :], weight[:, :, :]).then_inc(S("w_sig"), 1)
            dve.wait_ge(S("w_sig"), nth("w_sig", 1))
            dve.tensor_tensor(weight[:, :, :], weight[:, :, :], sel[:, :, :], ALU.mult).then_inc(S("w_sel"), 1)
            dve.wait_ge(S("w_sel"), nth("w_sel", 1))
            dve.tensor_reduce(rstd_all[:, :], weight[:, :, :], X_AXIS, ALU.add).then_inc(S("w_sum"), 1)
            dve.wait_ge(S("w_sum"), nth("w_sum", 1))
            dve.tensor_scalar(rstd_all[:, :], rstd_all[:, :], 1e-8, None, ALU.add).then_inc(S("w_sume"), 1)
            dve.wait_ge(S("w_sume"), nth("w_sume", 1))
            dve.reciprocal(rstd_all[:, :], rstd_all[:, :]).then_inc(S("w_inv"), 1)
            dve.wait_ge(S("w_inv"), nth("w_inv", 1))
            dve.tensor_tensor(weight[:, :, :], weight[:, :, :], rstd_all[:, :].unsqueeze(2).broadcast_to([P, NT, E1]), ALU.mult).then_inc(S("weight"), 1)
            dve.wait_ge(S("weight"), nth("weight", 1))

            def h1_T(n, k):
                j = n * RING + k
                p = k % 2
                dve.wait_ge(S("h1T_ps"), j + 1)
                if some(j - 1):
                    dve.wait_ge(S("dn1_ps"), j - 1)
                dve.tensor_copy(h1T[:, p, :], bank(4 + p)[:, 0:P]).then_inc(S("h1T"), 1)

            def out_x1(n, k):
                j = n * RING + k
                dve.wait_ge(S("dn1_ps"), j + 1)
                dve.wait_ge(S(f"rows_out{k}"), 16 * (n + GROUPS0))
                dve.tensor_copy(y1[:, k], bank(6 + k % 2)[:, 0:D]).then_inc(S("y1"), 1)

            def lag(step, n, k, d):
                k -= d
                if k >= 0:
                    step(n, k)
                elif not (isinstance(n, int) and n == 0):
                    step(n - 1, k + RING)

            def slot_weight(t, k):
                m = t * TOP1 + k
                if some(m - TOP1 + 1):
                    dve.wait_ge(S("w_slot"), m - TOP1 + 1)
                dve.scalar_tensor_tensor(slot_junk[:, k, :], row(slot_key, t), slots[:, bass.ts(m, 1)], row(weight, t), ALU.is_equal, ALU.mult,
                                         accum_out=w_slot[:, bass.ts(m, 1)]).then_inc(S("w_slot"), 1)

            def experts1(n, weights):
                for k in range(RING):
                    lag(h1_T, n, k, 1)
                    lag(out_x1, n, k, 2)
                    if weights:
                        slot_weight(n, k)
            experts1(0, True)
            with dve.Fori(1, NT, 1) as n:
                experts1(n, True)
            with dve.Fori(NT, GROUPS1, 1) as n:
                experts1(n, False)
            n = GROUPS1 - 1
            h1_T(n, RING - 1)
            out_x1(n, RING - 2)
            out_x1(n, RING - 1)
            dve.wait_ge(S("w_slot"), NT * TOP1)

            def combine(i):
                for half in range(2):
                    t = i * 2 + half
                    for k in range(TOP1):
                        if some(16 * (i + 1 + (1 - half) * (GROUPS0 + GROUPS1))):
                            dve.wait_ge(S(f"rows_in{RING * half + k}"), 16 * (i + 1 + (1 - half) * (GROUPS0 + GROUPS1)))
                        if some(TOP1 * t + k):
                            dve.wait_ge(S("acc"), TOP1 * t + k)
                        ins = dve.scalar_tensor_tensor(row(X, t), cg[:, half, k, :], w_slot[:, bass.ts(t * TOP1 + k, 1)], row(X, t), ALU.mult, ALU.add)
                        ins.then_inc(S("acc"), 1)
                    dve.wait_ge(S("acc"), TOP1 * (t + 1))
                    dve.sem_inc(S("final"), 1)
            combine(0)
            with dve.Fori(1, NT // 2, 1) as i:
                combine(i)

        @block.gpsimd
        def _(pool):
            pool.memset(ident[:, :], 0.0).then_inc(S("pool_const"), 1)
            pool.memset(tri[:, :], 0.0).then_inc(S("pool_const"), 1)
            pool.memset(triinc[:, :], 0.0).then_inc(S("pool_const"), 1)
            pool.memset(head_at, 0.0).then_inc(S("pool_const"), 1)
            pool.wait_ge(S("pool_const"), 4)
            pool.affine_select(out=head_at, in_=head_at, compare_op=ALU.not_equal, fill=1.0, base=0, pattern=[[-1, HG], [-HG, SL]], channel_multiplier=1).then_inc(S("pool_const"), 1)
            pool.affine_select(out=ident[:, :], in_=ident[:, :], compare_op=ALU.not_equal, fill=1.0, base=0, pattern=[[-1, P]], channel_multiplier=1).then_inc(S("pool_const"), 1)
            pool.affine_select(out=tri[:, :], in_=tri[:, :], compare_op=ALU.is_ge, fill=1.0, base=0, pattern=[[-1, P]], channel_multiplier=1).then_inc(S("pool_const"), 1)
            pool.affine_select(out=triinc[:, :], in_=triinc[:, :], compare_op=ALU.is_gt, fill=1.0, base=0, pattern=[[-1, P]], channel_multiplier=1).then_inc(S("pool_const"), 1)
            pool.iota(iota16[:, :], pattern=[[1, NX1]], base=0, channel_multiplier=0, allow_small_or_imprecise_dtypes=True).then_inc(S("pool_const"), 1)
            pool.iota(step128[:, :], pattern=[[P, NT]], base=0, channel_multiplier=0, allow_small_or_imprecise_dtypes=True).then_inc(S("pool_const"), 1)
            pool.iota(token_id[:, :], pattern=[[P, NT]], base=0, channel_multiplier=1, allow_small_or_imprecise_dtypes=True).then_inc(S("pool_const"), 1)
            pool.wait_ge(S("pool_const"), 11)
            pool.sem_inc(S("consts"), 1)
            pool.memset(one_col[:, :], 1.0).then_inc(S("log_scale"), 1)
            pool.memset(log_scale[:, :], math.log(QS)).then_inc(S("log_scale"), 1)
            pool.memset(vl[:, :, :, FD:VW], 1.0).then_inc(S("setup1_zeroed"), 1)
            pool.memset(vb[:, :, :, FD:VW], 1.0).then_inc(S("setup1_zeroed"), 1)
            pool.wait_ge(S("neg_half"), 1)
            pool.wait_ge(S("var1"), 1)
            pool.tensor_tensor(out=rstd_all[:, :], in0=rstd_all[:, :], in1=neg_half[:, :], op=ALU.pow).then_inc(S("rstd1"), 1)

            def power(name, t):
                pool.wait_ge(S("var" + name), nth("var" + name, t + 1))
                pool.tensor_tensor(out=rstd[:, :], in0=var_eps[:, :], in1=neg_half[:, 0:1], op=ALU.pow).then_inc(S("rstd" + name), 1)
            pool.memset(kbd, 0.0).then_inc(S("setup1_zeroed"), 1)
            power("2", 0)
            with pool.Fori(1, NT, 1) as t:
                power("2", t)

            def gathers(i, L, src, dst, before):
                for s in range(2):
                    n = i * 2 + s
                    for k in range(RING):
                        if some(n * 16 + 16 * (before - 1)):
                            pool.wait_ge(S(f"rows_in{k}"), n * 16 + 16 * (before - 1))
                    pool.tensor_copy(idx8[:, s, :], token_of[:, bass.ts(n, RING)]).then_inc(S(f"idx{L}"), 1)
                    pool.wait_ge(S(f"idx{L}"), n + 1)
                    for k in range(RING):
                        if some(n * RING + k - RING + 1):
                            pool.wait_ge(S(f"x{L}T_ps"), n * RING + k - RING + 1)
                        pool.sem_inc(S("waited_pool"), 1)
                        pool.indirect_dma_start(out=dst[:, k, :], out_offset=None, in_=src,
                                                in_offset=bass.IndirectOffsetOnAxis(ap=idx8[:, s, k:k + 1], axis=0)).then_inc(S(f"rows_in{k}"), 16)
            pool.wait_ge(S("table"), 1)
            pool.wait_ge(S("xs0_stored"), 16 * NT)
            gathers(0, 0, scaled0, g0, 0)
            with pool.Fori(1, GROUPS0 // 2, 1) as i:
                gathers(i, 0, scaled0, g0, 0)

            for k in range(RING):
                pool.wait_ge(S(f"rows_out{k}"), 16 * GROUPS0)

            def gather_y0(u):
                if some(u):
                    pool.wait_ge(S("x2"), nth("x2", u))
                pool.tensor_copy(idx1[:, :], slot_i[:, bass.ts(u, 1)]).then_inc(S("idx_y"), 1)
                pool.wait_ge(S("idx_y"), u + 1)
                pool.sem_inc(S("waited_pool"), 1)
                pool.indirect_dma_start(out=yg, out_offset=None, in_=routed0, in_offset=bass.IndirectOffsetOnAxis(ap=idx1[:, 0:1], axis=0)).then_inc(S("yg"), 16)

            gather_y0(0)
            power("3", 0)
            gather_y0(1)
            power("3", 1)
            gather_y0(2)

            def norms(t, behind=True, coming=True):
                if coming:
                    power("3", t + 2)
                    if not (isinstance(t, int) and t == NT - 3):
                        gather_y0(t + 3)
                if behind:
                    power("4", t - 1)
            norms(0, behind=False)
            norms(1)
            with pool.Fori(2, NT - 3, 1) as t:
                norms(t)
            for t in range(NT - 3, NT + 1):
                norms(t, coming=(t + 2 < NT))

            pool.wait_ge(S("table"), 2)
            gathers(0, 1, normed1, g1, GROUPS0)
            with pool.Fori(1, GROUPS1 // 2, 1) as i:
                gathers(i, 1, normed1, g1, GROUPS0)

            def combine(i):
                for half in range(2):
                    t = i * 2 + half
                    for k in range(TOP1):
                        if some(16 * (i + (1 - half) * (GROUPS0 + GROUPS1))):
                            pool.wait_ge(S(f"rows_in{RING * half + k}"), 16 * (i + (1 - half) * (GROUPS0 + GROUPS1)))
                    pool.tensor_copy(idx8[:, half, :], slot_i[:, bass.ts(t, TOP1)]).then_inc(S("idx_c"), 1)
                    pool.wait_ge(S("idx_c"), t + 1)
                    for k in range(TOP1):
                        if some(TOP1 * t + k - 2 * TOP1 + 1):
                            pool.wait_ge(S("acc"), TOP1 * t + k - 2 * TOP1 + 1)
                        pool.sem_inc(S("waited_pool"), 1)
                        pool.indirect_dma_start(out=cg[:, half, k, :], out_offset=None, in_=routed1,
                                                in_offset=bass.IndirectOffsetOnAxis(ap=idx8[:, half, k:k + 1], axis=0)).then_inc(S(f"rows_in{RING * half + k}"), 16)
            for k in range(RING):
                pool.wait_ge(S(f"rows_out{k}"), 16 * (GROUPS0 + GROUPS1))
            combine(0)
            with pool.Fori(1, NT // 2, 1) as i:
                combine(i)



_OUT = ((2, 1024, 256), "float32")


def _layout(inputs):
    import numpy as np
    a = {k: np.asarray(v) for k, v in inputs.items()}
    named = {
        "x": a["x"].reshape(-1, a["x"].shape[-1]),
        "ctxT": a["ctx_1024"].transpose(0, 2, 1),
        "mask": a["mask_SxS2_fk1"],
        "WqT": a["L0_xattn_Wq"].T, "bq": a["L0_xattn_bq"].reshape(-1, P).T,
        "Wk": a["L0_xattn_Wk"], "bk": a["L0_xattn_bk"].reshape(-1, P).T,
        "Wv": a["L0_xattn_Wv"], "bv": a["L0_xattn_bv"],
        "w_routerT": a["L0_ffn_w_router"].T,
        "gate_up": a["L0_ffn_gate_up_proj"], "down": a["L0_ffn_down_proj"],
        "w_gateT": a["L0_ffn_w_gate"].T, "w_upT": a["L0_ffn_w_up"].T, "w_downT": a["L0_ffn_w_down"].T,
        "fm_wT": a["L1_xattn_fm_w"].T, "fm_b": a["L1_xattn_fm_b"],
        "fc_wT": a["L1_xattn_fc_w"].T, "fc_b": a["L1_xattn_fc_b"],
        "centroidsT": a["L1_ffn_centroids"].T, "expert_biases": a["L1_ffn_expert_biases"],
        "Ws_up": a["L1_ffn_Ws_up"], "Ws_down": a["L1_ffn_Ws_down"],
        "W_up": a["L1_ffn_W_up"], "W_down": a["L1_ffn_W_down"],
    }
    return {k: np.ascontiguousarray(v) for k, v in named.items()}


def kernel(**inputs):
    import concourse.bacc as bacc
    from concourse.bass_utils import run_bass_kernel_spmd as run

    nc = bacc.Bacc("TRN2", target_bir_lowering=False, num_devices=1)
    arrays, args = {}, {}
    for name, a in _layout(inputs).items():
        arrays[f"in_{name}"] = a
        args[name] = nc.dram_tensor(f"in_{name}", a.shape, mybir.dt.from_np(a.dtype), kind="ExternalInput").ap()
    result = nc.dram_tensor("out_x", [_OUT[0][0] * _OUT[0][1], _OUT[0][2]], F32, kind="ExternalOutput").ap()
    build(nc, **args, out=result)
    r = run(nc, [arrays], core_ids=[0])
    return r.results[0]["out_x"].reshape(_OUT[0])
```
